# Optimizing a Trainium2 kernel written in Bass

```python
import numpy as np
import jax
import jax.numpy as jnp

def _softmax(x, axis=-1):
    return jax.nn.softmax(x, axis=axis)

def _gelu(x):
    return jax.nn.gelu(x, approximate=True)

def _silu(x):
    return jax.nn.silu(x)

def _sigmoid(x):
    return jax.nn.sigmoid(x)

def _layernorm(x, axis=-1, eps=1e-05):
    m = jnp.mean(x, axis=axis, keepdims=True)
    v = jnp.var(x, axis=axis, keepdims=True)
    return (x - m) / jnp.sqrt(v + eps)

def _scatter_add(tgt, idx, src, axis=0):
    return tgt.at[idx].add(src)

def _segment_sum(src, seg, n):
    return jax.ops.segment_sum(src, seg, n)
kernel_name = 'mk_flamingo_gated_d1_seqx_r4_f9837e'

def setup_inputs(seed: int=0):
    np.random.seed(seed)
    _w = jnp.asarray

    def _rec_inputs():
        import jax
        import jax.numpy as jnp
        _rk = jax.random.key(seed)
        x = -0.0002928 + 1 * jax.random.normal(jax.random.fold_in(_rk, 1), (4, 1024, 256), jnp.float32)
        _lenS = 1024 - jax.random.randint(jax.random.fold_in(_rk, 7), (4,), 0, max(1, 1024 // 4) + 1, jnp.int32)
        _lenS2 = 77 - jax.random.randint(jax.random.fold_in(_rk, 8), (4,), 0, max(1, 77 // 4) + 1, jnp.int32)
        _ctx_1024P = jax.random.normal(jax.random.fold_in(_rk, 11), (4, 16, 256), jnp.float32)
        _ctx_1024c = jax.random.dirichlet(jax.random.fold_in(_rk, 511), 0.3 * jnp.ones((16,), jnp.float32), (4, 77))
        _ctx_1024t = jnp.einsum('bsk,bkd->bsd', _ctx_1024c, _ctx_1024P)
        _ctx_1024t = _ctx_1024t * jax.lax.rsqrt(jnp.mean(jnp.square(_ctx_1024t)) + 1e-12) * 0.953939
        ctx_1024 = -1.39393e-06 + 0.999914 * (_ctx_1024t + 0.3 * jax.random.normal(jax.random.fold_in(_rk, 611), (4, 77, 256), jnp.float32))
        _validS = jnp.arange(1024)[None, :] < _lenS[:, None]
        _validS2 = jnp.arange(77)[None, :] < _lenS2[:, None]
        _causal = jnp.tril(jnp.ones((1024, 1024), dtype=bool))
        mask_BxS2_bf1 = jnp.ones((4, 77), dtype=bool)
        _g = jax.random.normal(jax.random.fold_in(_rk, 9001), (2, 1), jnp.float32)
        _g = jnp.sign(_g) * jnp.maximum(jnp.abs(_g), 1.0) + (_g == 0) * 1.0
        g_xattn = _g[0]
        g_ffn = _g[1]
        return (x, ctx_1024, mask_BxS2_bf1, g_xattn, g_ffn)
    x, ctx_1024, mask_BxS2_bf1, g_xattn, g_ffn = _rec_inputs()

    def _L0_xattn_setup():
        import jax, jax.numpy as jnp
        import numpy as np
        B, N, HID, HEADS, TOPK = (2, 512, 256, 16, 64)
        DHEAD = HID // HEADS

        def _split_heads(x):
            b, n, _ = x.shape
            return x.reshape(b, n, HEADS, DHEAD).transpose(0, 2, 1, 3)
        key = jax.random.key(seed)
        ks = jax.random.split(key, 12)
        s = 1.0 / np.sqrt(HID)
        inp = {'q': jax.random.normal(ks[0], (B, N, HID), jnp.float32), 'k': jax.random.normal(ks[1], (B, N, HID), jnp.float32), 'v': jax.random.normal(ks[2], (B, N, HID), jnp.float32), 'mask': jnp.ones((B, N), jnp.bool_), 'topk': TOPK, 'wq_w': jax.random.normal(ks[3], (HID, HID), jnp.float32) * s, 'wq_b': jnp.zeros((HID,), jnp.float32), 'wk_w': jax.random.normal(ks[4], (HID, HID), jnp.float32) * s, 'wk_b': jnp.zeros((HID,), jnp.float32), 'wv_w': jax.random.normal(ks[5], (HID, HID), jnp.float32) * s, 'wv_b': jnp.zeros((HID,), jnp.float32), 'wo_w': jax.random.normal(ks[6], (HID, HID), jnp.float32) * s, 'wo_b': jnp.zeros((HID,), jnp.float32)}
        return inp
    _L0_xattn_all = _L0_xattn_setup()
    _L0_xattn_in = {k: v for k, v in _L0_xattn_all.items() if k in ('wq_w', 'wq_b', 'wk_w', 'wk_b', 'wv_w', 'wv_b', 'wo_w', 'wo_b')}
    del _L0_xattn_all

    def _L0_ffn_setup():
        import jax, jax.numpy as jnp
        import numpy as np
        from jax import lax
        T, B, I, M, O = (64, 64, 256, 256, 256)

        def _xavier(key, shape):
            fan_out, fan_in = shape
            limit = float(np.sqrt(6.0 / (fan_in + fan_out)))
            return jax.random.uniform(key, shape, jnp.float32, -limit, limit)
        key = jax.random.key(seed)
        ks = jax.random.split(key, 9)
        x = jax.random.normal(ks[0], (T, B, I), jnp.float32)
        return {'x': x, 'wf': _xavier(ks[1], (M, I)), 'uf': _xavier(ks[2], (M, M)), 'bf': jnp.zeros((M,), jnp.float32), 'wi': _xavier(ks[3], (M, I)), 'ui': _xavier(ks[4], (M, M)), 'bi': jnp.zeros((M,), jnp.float32), 'wc': _xavier(ks[5], (M, I)), 'uc': _xavier(ks[6], (M, M)), 'bc': jnp.zeros((M,), jnp.float32), 'wo': _xavier(ks[7], (O, I)), 'uo': _xavier(ks[8], (O, M)), 'bo': jnp.zeros((O,), jnp.float32), 'in_c': jnp.zeros((M,), jnp.float32)}
    _L0_ffn_all = _L0_ffn_setup()
    _L0_ffn_in = {k: v for k, v in _L0_ffn_all.items() if k in ('wf', 'uf', 'bf', 'wi', 'ui', 'bi', 'wc', 'uc', 'bc', 'wo', 'uo', 'bo', 'in_c')}
    del _L0_ffn_all
    return {'x': x, 'ctx_1024': ctx_1024, 'mask_BxS2_bf1': mask_BxS2_bf1, 'g_xattn': g_xattn, 'g_ffn': g_ffn, 'L0_xattn_wq_w': _L0_xattn_in['wq_w'], 'L0_xattn_wq_b': _L0_xattn_in['wq_b'], 'L0_xattn_wk_w': _L0_xattn_in['wk_w'], 'L0_xattn_wk_b': _L0_xattn_in['wk_b'], 'L0_xattn_wv_w': _L0_xattn_in['wv_w'], 'L0_xattn_wv_b': _L0_xattn_in['wv_b'], 'L0_xattn_wo_w': _L0_xattn_in['wo_w'], 'L0_xattn_wo_b': _L0_xattn_in['wo_b'], 'L0_ffn_wf': _L0_ffn_in['wf'], 'L0_ffn_uf': _L0_ffn_in['uf'], 'L0_ffn_bf': _L0_ffn_in['bf'], 'L0_ffn_wi': _L0_ffn_in['wi'], 'L0_ffn_ui': _L0_ffn_in['ui'], 'L0_ffn_bi': _L0_ffn_in['bi'], 'L0_ffn_wc': _L0_ffn_in['wc'], 'L0_ffn_uc': _L0_ffn_in['uc'], 'L0_ffn_bc': _L0_ffn_in['bc'], 'L0_ffn_wo': _L0_ffn_in['wo'], 'L0_ffn_uo': _L0_ffn_in['uo'], 'L0_ffn_bo': _L0_ffn_in['bo'], 'L0_ffn_in_c': _L0_ffn_in['in_c']}

def reference(x, ctx_1024, mask_BxS2_bf1, g_xattn, g_ffn, L0_xattn_wq_w, L0_xattn_wq_b, L0_xattn_wk_w, L0_xattn_wk_b, L0_xattn_wv_w, L0_xattn_wv_b, L0_xattn_wo_w, L0_xattn_wo_b, L0_ffn_wf, L0_ffn_uf, L0_ffn_bf, L0_ffn_wi, L0_ffn_ui, L0_ffn_bi, L0_ffn_wc, L0_ffn_uc, L0_ffn_bc, L0_ffn_wo, L0_ffn_uo, L0_ffn_bo, L0_ffn_in_c):
    import jax
    import jax.numpy as jnp

    def _L0_xattn_ref(q, k, v, mask, topk, wq_w, wq_b, wk_w, wk_b, wv_w, wv_b, wo_w, wo_b):
        import jax, jax.numpy as jnp
        import numpy as np
        B, N, HID, HEADS, TOPK = (2, 512, 256, 16, 64)
        DHEAD = HID // HEADS

        def _split_heads(x):
            b, n, _ = x.shape
            return x.reshape(b, n, HEADS, DHEAD).transpose(0, 2, 1, 3)
        qh = _split_heads(q @ wq_w.T + wq_b)
        kh = _split_heads(k @ wk_w.T + wk_b)
        vh = _split_heads(v @ wv_w.T + wv_b)
        scores = jnp.einsum('bhqd,bhkd->bhqk', qh, kh) / np.sqrt(DHEAD)
        neg = jnp.finfo(scores.dtype).min
        scores = jnp.where(mask[:, None, None, :], scores, neg)
        if topk and 0 < topk < scores.shape[-1]:
            vals, idx = jax.lax.top_k(scores, topk)
            b, h, nq, _ = scores.shape
            bI = jnp.arange(b)[:, None, None, None]
            hI = jnp.arange(h)[None, :, None, None]
            qI = jnp.arange(nq)[None, None, :, None]
            scores = jnp.full_like(scores, neg).at[bI, hI, qI, idx].set(vals)
        probs = jax.nn.softmax(scores, axis=-1)
        ctx = jnp.einsum('bhqk,bhkd->bhqd', probs, vh)
        ctx = ctx.transpose(0, 2, 1, 3).reshape(q.shape[0], q.shape[1], HID)
        return ctx @ wo_w.T + wo_b

    def _L0_ffn_ref(x, wf, uf, bf, wi, ui, bi, wc, uc, bc, wo, uo, bo, in_c):
        import jax, jax.numpy as jnp
        import numpy as np
        from jax import lax
        T, B, I, M, O = (64, 64, 256, 256, 256)

        def _xavier(key, shape):
            fan_out, fan_in = shape
            limit = float(np.sqrt(6.0 / (fan_in + fan_out)))
            return jax.random.uniform(key, shape, jnp.float32, -limit, limit)
        batch = x.shape[1]
        c0 = jnp.broadcast_to(in_c, (batch, in_c.shape[0]))

        def step(c, xt):
            ft = jax.nn.sigmoid(xt @ wf.T + c @ uf.T + bf)
            it = jax.nn.sigmoid(xt @ wi.T + c @ ui.T + bi)
            gt = jnp.tanh(xt @ wc.T + c @ uc.T + bc)
            c = ft * c + it * gt
            return (c, None)
        c_final, _ = lax.scan(step, c0, x)
        h = jnp.tanh(jnp.einsum('tbi,oi->tbo', x, wo) + c_final @ uo.T + bo)
        return h
    x = x + jnp.tanh(g_xattn[0]) * _L0_xattn_ref(_layernorm(x, axis=-1), ctx_1024, ctx_1024, mask_BxS2_bf1, 64, L0_xattn_wq_w, L0_xattn_wq_b, L0_xattn_wk_w, L0_xattn_wk_b, L0_xattn_wv_w, L0_xattn_wv_b, L0_xattn_wo_w, L0_xattn_wo_b)
    x = x + jnp.tanh(g_ffn[0]) * _L0_ffn_ref(_layernorm(x, axis=-1), L0_ffn_wf, L0_ffn_uf, L0_ffn_bf, L0_ffn_wi, L0_ffn_ui, L0_ffn_bi, L0_ffn_wc, L0_ffn_uc, L0_ffn_bc, L0_ffn_wo, L0_ffn_uo, L0_ffn_bo, L0_ffn_in_c)
    return x

_drawn_inputs = setup_inputs


def setup_inputs(seed=0):
    import zlib

    import numpy as np

    out = dict(_drawn_inputs(seed))
    spreads = {'L0_xattn_wq_b': (0.0, 0.448),
     'L0_xattn_wk_b': (0.0, 0.8),
     'L0_xattn_wv_b': (0.0, 0.1),
     'L0_xattn_wo_b': (0.0, 0.1),
     'L0_ffn_bf': (0.0, 0.8),
     'L0_ffn_bi': (0.0, 0.8),
     'L0_ffn_bc': (0.0, 0.1),
     'L0_ffn_bo': (0.0, 0.1),
     'L0_ffn_in_c': (0.0, 0.542)}
    factors = {}
    for name, (base, spread) in spreads.items():
        noise = np.random.default_rng([zlib.crc32(name.encode()), seed]).standard_normal(out[name].shape)
        drawn = base * np.exp(spread * noise) if base else spread * noise
        out[name] = jnp.asarray(drawn.astype(out[name].dtype))
    for name, factor in factors.items():
        out[name] = (out[name] * factor).astype(out[name].dtype)
    return out
```

```python
from contextlib import ExitStack

import concourse.bass as bass
from concourse import mybir

ALU = mybir.AluOpType
ACT = mybir.ActivationFunctionType
AX = mybir.AxisListType
F32 = mybir.dt.float32
BF16 = mybir.dt.bfloat16
U8 = mybir.dt.uint8

P = 128
B, N, D, H, DH, NK, TOPK = 4, 1024, 256, 16, 16, 77, 64
KD = D // P
T = B * N // P
IT = T // 2
IB = N // (2 * P)
HK = H * NK
DROP = NK - TOPK
HB = 6
HC = P // DH
KC = (HK + P - 1) // P
VW = 3 * (DH + 1)
BIG = 2.0 ** 126
EPS = 1e-5


def chunk_heads(c):
    first = c * P // NK
    return first, (min((c + 1) * P, HK) - 1) // NK - first + 1


def rows(c):
    return min(P, HK - c * P)


def at_least(eng, sem, n, most=None):
    if isinstance(n, int):
        if most is not None:
            n = min(n, most)
        if n <= 0:
            return
    eng.wait_ge(sem, n)


def hold(eng, held, sem, n, most=None):
    if isinstance(n, int):
        at_least(eng, sem, n, most)
        return
    eng.wait_ge(sem, n)
    eng.sem_inc(held, 1)


def pipeline(eng, slot, first, last, begin, end):
    for i in range(first, begin):
        for u in range(2):
            slot(i, u)
    with eng.Fori(begin, end) as i:
        for u in range(2):
            slot(i, u)
    for i in range(end, last):
        for u in range(2):
            slot(i, u)


def end_steps(eng, step):
    for u in range(2):
        step(0, u)
    with eng.Fori(1, IT // 2) as n:
        for u in range(2):
            step(n, u)


def there(t, n=T):
    return not isinstance(t, int) or 0 <= t < n


FIRST, LAST = -2, IT + 3
BEGIN, END = 3, IT - 2


def build(nc, x, ctxT, mask, w_attn, w_ffn, cols, brows, gates, out):
    x_rows = x.rearrange("b n d -> (b n) d")
    out_rows = out.rearrange("b n d -> (b n) d")
    with ExitStack() as stack:
        def sb(name, shape, dt=F32):
            return stack.enter_context(nc.sbuf_tensor(name, shape, dt))

        def ps(name, shape, dt=F32):
            return stack.enter_context(nc.psum_tensor(name, shape, dt))

        def sem(name):
            return stack.enter_context(nc.semaphore(name))

        xres = sb("xres", [P, T, D])
        hpre = sb("hpre", [P, IT, KD * 2 * P])
        state = sb("state", [P, KD, N])
        kbd = sb("kbd", [P, B, KD, HC, NK])
        vbd = sb("vbd", [P, B, KC, VW])
        wa = sb("wa", [P, 4, KD, D])
        wf = sb("wf", [P, 8, KD, D])
        col = sb("col", [P, 7, KD])
        half = sb("half", [P, 7, KD])
        kbias = sb("kbias", [P, KD])
        brow = sb("brow", [P, 2, D])
        gcol = sb("gcol", [P, 2])
        tg = sb("tg", [P, 2])
        tgbo = sb("tgbo", [P, D])
        ident = sb("ident", [P, P])
        mask8 = sb("mask8", [P, B, NK], U8)
        mbias = sb("mbias", [P, B, NK], BF16)
        first_row = sb("first_row", [P, P], BF16)
        anyk = sb("anyk", [P, B])
        escale = sb("escale", [P, B])
        minus_half = sb("minus_half", [P, 1])
        st1, mv1, ve1, rs1 = sb("st1", [P, 6]), sb("mv1", [P, 2]), sb("ve1", [P, 1]), sb("rs1", [P, 1])
        st2, mv2, ve2, rs2 = sb("st2", [P, 6]), sb("mv2", [P, 2]), sb("ve2", [P, 1]), sb("rs2", [P, 1])
        xhat = sb("xhat", [P, 2, D])
        xT = sb("xT", [P, KD, 2, P])
        qT = sb("qT", [P, KD, 2, P])
        raw = sb("raw", [P, 2, H, NK])
        neg = sb("neg", [P, 2, H, NK])
        left = sb("left", [P, H, NK])
        kept = sb("kept", [P, 2, H, NK])
        negmin = sb("negmin", [P, 2, H])
        top1 = sb("top1", [P, H, 8])
        top2 = sb("top2", [P, H, 8])
        probT = sb("probT", [P, 2, KC, P])
        rden = sb("rden", [P, H])
        ctxn = sb("ctxn", [P, 2, D])
        ctxnT = sb("ctxnT", [P, 2, KD, P])
        yhat = sb("yhat", [P, 2, D])
        yT = sb("yT", [P, KD, 2, P])
        gate_in = sb("gate_in", [P, 3, KD * 2 * P])
        sig = sb("sig", [P, 2, KD * 2 * P])
        sel = left[0:NK].rearrange("k h n -> k (h n)")
        keysT = probT[:, 0, 0:5, :].rearrange("p c n -> p (c n)")[:, 0:KD * B * NK]
        keysT = keysT.rearrange("p (m b n) -> p m b n", m=KD, b=B)
        vals = probT[0:NK, 1, 0:8, :].rearrange("p c n -> p (c n)").rearrange("p (b d) -> p b d", b=B)
        ctx_in = neg[:, 0, :, :].rearrange("p h n -> p (h n)")[:, 0:KD * B * NK]
        ctx_in = ctx_in.rearrange("p (k n) -> p k n", k=KD)
        spare = raw[:, 1].rearrange("p h n -> p (h n)")
        hmask = spare[:, 0:KC * H].rearrange("p (c h) -> p c h", h=H)
        cmask = spare[:, KC * H:KC * H + HC]
        ustate = raw
        ustate_v = raw[:, :, :, :].rearrange("p u h n -> p (u h n)")[:, 0:IB * KD * 2 * P]
        ustate_v = ustate_v.rearrange("p (j n) -> p j n", j=IB)
        hsum = neg[:, :, 0:7, :].rearrange("p u h n -> p u (h n)")[:, :, 0:KD * 2 * P]
        hT = kept[:, :, 0:7, :].rearrange("p u h n -> p u (h n)")[:, :, 0:KD * 2 * P]
        fin = sb("fin", [P, 2, 2 * D])

        s_ps = ps("s_ps", [P, 3, 512])
        pt_ps = [ps(f"pt_ps{n}", [P, 512]) for n in range(2)]
        c_ps = ps("c_ps", [P, 512])
        o_ps = ps("o_ps", [P, 512])
        g_ps = ps("g_ps", [P, 512])

        w_in, ctx_come, ffn_come = sem("w_in"), sem("ctx_come"), sem("ffn_come")
        x_in, held = sem("x_in"), sem("held")
        row_set = sem("row_set")
        pool_set, dve_set, act_set = sem("pool_set"), sem("dve_set"), sem("act_set")
        keys_ps, keys_sb, kbd_set = sem("keys_ps"), sem("keys_sb"), sem("kbd_set")
        vals_ps, vals_sb = sem("vals_ps"), sem("vals_sb")
        vrow_ps, vrow_sb = sem("vrow_ps"), sem("vrow_sb")
        ln1_stat, ln1_var, ln1_eps, rstd1 = sem("ln1_stat"), sem("ln1_var"), sem("ln1_eps"), sem("rstd1")
        ln2_stat, ln2_var, ln2_eps, rstd2 = sem("ln2_stat"), sem("ln2_var"), sem("ln2_eps"), sem("rstd2")
        xhat_in, xT_ps, xT_in = sem("xhat_in"), sem("xT_ps"), sem("xT_in")
        q_ps, q_in = sem("q_ps"), sem("q_in")
        score_ps, raw_in, neg_in = sem("score_ps"), sem("raw_in"), sem("neg_in")
        min_in, top1_in, left_in, top2_in, top2_cut, kept_in = (
            sem("min_in"), sem("top1_in"), sem("left_in"), sem("top2_in"), sem("top2_cut"), sem("kept_in"))
        mag_in = sem("mag_in")
        probT_ps, probT_in, ctx_ps, rden_in, ctxn_in = (
            sem("probT_ps"), sem("probT_in"), sem("ctx_ps"), sem("rden_in"), sem("ctxn_in"))
        ctxT_ps, ctxT_in, attn_ps, biased, x2_in = (
            sem("ctxT_ps"), sem("ctxT_in"), sem("attn_ps"), sem("biased"), sem("x2_in"))
        yhat_in, yT_ps, yT_in = sem("yhat_in"), sem("yT_ps"), sem("yT_in")
        gate_ps, gate_done, sig_in, fresh_in, state_in = (
            sem("gate_ps"), sem("gate_done"), sem("sig_in"), sem("fresh_in"), sem("state_in"))
        u_ps, u_in, hsum_in, h_in, hT_ps, fin_in = (
            sem("u_ps"), sem("u_in"), sem("hsum_in"), sem("h_in"), sem("hT_ps"), sem("fin_in"))
        stored = [sem(f"stored{u}") for u in range(2)]

        block = stack.enter_context(nc.Block())

        @block.sync
        def _(sp):
            sp.dma_start(ctx_in, ctxT.rearrange("(k p) n -> p k n", p=P)).then_inc(ctx_come, 16)
            sp.dma_start(mask8[:], mask.rearrange("p (b n) -> p b n", b=B)).then_inc(w_in, 16)
            sp.dma_start(col[:], cols.rearrange("p (a k) -> p a k", k=KD)).then_inc(w_in, 16)
            sp.dma_start(brow[:], brows).then_inc(w_in, 16)
            sp.dma_start(gcol[:], gates).then_inc(w_in, 16)
            sp.dma_start(wa[:], w_attn.rearrange("a (k p) n -> p a k n", p=P)).then_inc(w_in, 16)

            def load(i):
                sp.dma_start(xres[:, bass.ds(2 * i, 2), :],
                             x_rows[bass.ds(2 * P * i, 2 * P), :].rearrange("(u p) d -> p u d", p=P)
                             ).then_inc(x_in, 16)
                hold(sp, held, x_in, 16 * i + 16)

            load(0)
            sp.dma_start(wf[:], w_ffn.rearrange("a (k p) n -> p a k n", p=P)).then_inc(ffn_come, 16)
            with sp.Fori(1, IT) as i:
                load(i)

            def store(n, u):
                hold(sp, held, fin_in, 2 * n + u + 1)
                sp.dma_start(out_rows[bass.ds(2 * P * (2 * n + u), 2 * P), :]
                             .rearrange("(u p) d -> p u d", p=P),
                             fin[:, u, :].rearrange("p (u d) -> p u d", u=2)).then_inc(stored[u], 16)

            end_steps(sp, store)
            for u in range(2):
                sp.wait_ge(stored[u], 16 * (IT // 2))

        @block.gpsimd
        def _(pool):
            nc.gpsimd.memset(ident[:], 0.0).then_inc(pool_set, 1)
            nc.gpsimd.memset(cmask, 1.0).then_inc(pool_set, 1)
            nc.gpsimd.memset(hmask, 1.0).then_inc(pool_set, 1)
            nc.gpsimd.memset(minus_half[:], -0.5).then_inc(pool_set, 1)
            nc.gpsimd.memset(first_row[:], 0.0).then_inc(row_set, 1)
            pool.wait_ge(row_set, 1)
            nc.gpsimd.memset(first_row[0:1], 1.0).then_inc(row_set, 1)
            pool.wait_ge(pool_set, 4)
            nc.gpsimd.affine_select(out=ident[:], in_=ident[:], compare_op=ALU.not_equal, fill=1.0, base=0,
                                    pattern=[[-1, P]], channel_multiplier=1).then_inc(pool_set, 1)
            nc.gpsimd.affine_select(out=cmask, in_=cmask, compare_op=ALU.is_ge, fill=0.0, base=0,
                                    pattern=[[-DH, HC]], channel_multiplier=1).then_inc(pool_set, 1)
            nc.gpsimd.affine_select(out=hmask, in_=hmask, compare_op=ALU.is_ge, fill=0.0, base=0,
                                    pattern=[[P, KC], [-NK, H]], channel_multiplier=1).then_inc(pool_set, 1)
            pool.wait_ge(pool_set, 7)
            nc.gpsimd.affine_select(out=cmask, in_=cmask, compare_op=ALU.is_ge, fill=0.0, base=DH - 1,
                                    pattern=[[DH, HC]], channel_multiplier=-1).then_inc(pool_set, 1)
            nc.gpsimd.affine_select(out=hmask, in_=hmask, compare_op=ALU.is_ge, fill=0.0, base=NK - 1,
                                    pattern=[[-P, KC], [NK, H]], channel_multiplier=-1).then_inc(pool_set, 1)
            pool.wait_ge(pool_set, 9)
            for c in range(KC):
                h0, nh = chunk_heads(c)
                ones = vbd[:, :, c, :].rearrange("p b (h d) -> p b h d", d=DH + 1)[:, :, 0:nh, DH]
                nc.gpsimd.tensor_copy(ones, hmask[:, c:c + 1, h0:h0 + nh].broadcast_to([P, B, nh])
                                      ).then_inc(pool_set, 1)
            pool.wait_ge(keys_sb, KD)
            for b in range(1, B):
                for m in range(KD):
                    nc.gpsimd.tensor_tensor(kbd[:, b, m], keysT[:, m, b:b + 1, :].broadcast_to([P, HC, NK]),
                                            cmask.rearrange("p (h o) -> p h o", o=1).broadcast_to([P, HC, NK]),
                                            ALU.mult).then_inc(kbd_set, 1)
            pool.wait_ge(dve_set, 6)

            def inverse_deviation(t, mv, ve, rs, var_in, eps_in, rstd):
                hold(pool, held, var_in, t + 1)
                nc.gpsimd.tensor_scalar(ve[:], mv[:, 1:2], EPS, None, ALU.add).then_inc(eps_in, 1)
                at_least(pool, eps_in, t + 1)
                nc.gpsimd.tensor_tensor(rs[:], ve[:], minus_half[:], ALU.pow).then_inc(rstd, 1)

            def slot(i, u):
                t = 2 * i + u
                k = i - 3
                if u == 0 and there(k, IT):
                    c_now = state[:, :, bass.ds((k % IB) * 2 * P, 2 * P)]
                    hold(pool, held, gate_done, 4 * k + 3)
                    nc.gpsimd.tensor_scalar(sig[:], gate_in[:, 0:2], 0.5, 0.5, ALU.mult, ALU.add
                                            ).then_inc(sig_in, 1)
                    hold(pool, held, sig_in, k + 1)
                    nc.gpsimd.tensor_tensor(sig[:, 0].rearrange("p (k n) -> p k n", k=KD),
                                            sig[:, 0].rearrange("p (k n) -> p k n", k=KD), c_now, ALU.mult
                                            ).then_inc(fresh_in, 1)
                    nc.gpsimd.tensor_tensor(sig[:, 1], sig[:, 1], gate_in[:, 2], ALU.mult
                                            ).then_inc(fresh_in, 1)
                    at_least(pool, gate_ps, 4 * k + 3)
                    hold(pool, held, fresh_in, 2 * k + 2)
                    nc.gpsimd.tensor_tensor(c_now, sig[:, 0].rearrange("p (k n) -> p k n", k=KD),
                                            sig[:, 1].rearrange("p (k n) -> p k n", k=KD), ALU.add
                                            ).then_inc(state_in, 1)
                if there(t + 4):
                    inverse_deviation(t + 4, mv1, ve1, rs1, ln1_var, ln1_eps, rstd1)
                if there(t - 2):
                    inverse_deviation(t - 2, mv2, ve2, rs2, ln2_var, ln2_eps, rstd2)
                if there(t + 1):
                    s, v = t + 1, 1 - u
                    at_least(pool, left_in, s - 1)
                    at_least(pool, min_in, s + 1)
                    nc.gpsimd.tensor_tensor(neg[:, v], raw[:, v],
                                            negmin[:, v].rearrange("p (h o) -> p h o", o=1)
                                            .broadcast_to([P, H, NK]), ALU.add).then_inc(neg_in, 1)
                if there(t + 3):
                    s = t + 3
                    hold(pool, held, xhat_in, s + 1)
                    nc.gpsimd.tensor_tensor(xres[:, bass.ds(s, 1), :], xres[:, bass.ds(s, 1), :],
                                            tgbo[:].rearrange("p (o d) -> p o d", o=1), ALU.add
                                            ).then_inc(biased, 1)

            pipeline(pool, slot, FIRST, LAST + 1, BEGIN, END)

            pool.wait_ge(left_in, T)
            pool.wait_ge(gate_done, 4 * IT)
            pool.wait_ge(u_in, IB)

            def add_parts(n, u):
                k = 2 * n + u
                hold(pool, held, h_in, k - 1)
                nc.gpsimd.tensor_tensor(hsum[:, u:u + 1], hpre[:, bass.ds(k, 1)],
                                        ustate_v[:, bass.ds(k % IB, 1)], ALU.add).then_inc(hsum_in, 1)

            end_steps(pool, add_parts)

        @block.vector
        def _(dve):
            dve.wait_ge(w_in, 80)
            nc.vector.tensor_scalar(kbias[:], col[:, 1], -0.25, None, ALU.mult).then_inc(dve_set, 1)
            nc.vector.tensor_scalar(half[:], col[:], 0.5, None, ALU.mult).then_inc(dve_set, 1)
            nc.vector.tensor_scalar(mbias[:], mask8[:], -BIG, BIG, ALU.mult, ALU.add).then_inc(dve_set, 1)
            nc.vector.tensor_reduce(anyk[:], mask8[:], AX.X, ALU.max).then_inc(dve_set, 1)
            dve.wait_ge(dve_set, 4)
            nc.vector.tensor_scalar(escale[:], anyk[:], -1.0, None, ALU.mult).then_inc(dve_set, 1)
            for j in range(IB):
                nc.vector.tensor_copy(state[:, :, j * 2 * P:(j + 1) * 2 * P],
                                      col[:, 6, :].rearrange("p (k o) -> p k o", o=1)
                                      .broadcast_to([P, KD, 2 * P])).then_inc(state_in, 1)
            dve.wait_ge(act_set, 1)
            nc.vector.tensor_scalar(tgbo[:], brow[:, 1], tg[:, 0:1], None, ALU.mult).then_inc(dve_set, 1)
            dve.wait_ge(pool_set, 9)
            nc.vector.tensor_copy(left[0:NK], ident[0:NK, 0:NK].rearrange("p (o n) -> p o n", o=1)
                                  .broadcast_to([NK, H, NK])).then_inc(dve_set, 1)
            dve.wait_ge(keys_sb, KD)
            for m in range(KD):
                nc.vector.tensor_tensor(kbd[:, 0, m], keysT[:, m, 0:1, :].broadcast_to([P, HC, NK]),
                                        cmask.rearrange("p (h o) -> p h o", o=1).broadcast_to([P, HC, NK]),
                                        ALU.mult).then_inc(kbd_set, 1)
            for b in range(B):
                dve.wait_ge(vals_ps, b + 1)
                nc.vector.tensor_tensor(vals[:, b], (c_ps if b % 2 else o_ps)[0:NK, 0:D], brow[0:NK, 0], ALU.add
                                        ).then_inc(vals_sb, 1)
            for c in range(KC):
                h0, nh = chunk_heads(c)
                dve.wait_ge(vrow_ps, c + 1)
                v_out = vbd[0:rows(c), :, c, :].rearrange("p b (h d) -> p b h d", d=DH + 1)[:, :, 0:nh, 0:DH]
                v_in = (c_ps if c % 2 else o_ps)[0:rows(c), 0:B * nh * DH]
                nc.vector.tensor_tensor(v_out, v_in.rearrange("p (b h d) -> p b h d", b=B, d=DH),
                                        hmask[0:rows(c), c:c + 1, h0:h0 + nh].rearrange("p o (h d) -> p o h d", d=1)
                                        .broadcast_to([rows(c), B, nh, DH]), ALU.mult).then_inc(vrow_sb, 1)

            def slot(i, u):
                t = 2 * i + u
                if there(t):
                    hold(dve, held, neg_in, t + 1)
                    for h in range(H):
                        mx = nc.vector.max(top1[:, h], neg[:, u, h])
                    mx.then_inc(top1_in, 1)
                if there(t - 2):
                    s = t - 2
                    at_least(dve, biased, s + 1)
                    at_least(dve, attn_ps, s + 1)
                    nc.vector.scalar_tensor_tensor(xres[:, bass.ds(s, 1), :],
                                                   o_ps[:, D:2 * D].rearrange("p (o d) -> p o d", o=1),
                                                   tg[:, 0:1], xres[:, bass.ds(s, 1), :], ALU.mult, ALU.add
                                                   ).then_inc(x2_in, 1)
                if there(t + 4):
                    s = t + 4
                    hold(dve, held, x_in, 16 * (i + 3))
                    nc.vector.bn_stats(st1[:], xres[:, bass.ds(s, 1), :]).then_inc(ln1_stat, 1)
                if there(t - 2):
                    s = t - 2
                    hold(dve, held, x2_in, s + 1)
                    nc.vector.bn_stats(st2[:], xres[:, bass.ds(s, 1), :]).then_inc(ln2_stat, 1)
                if there(t + 4):
                    hold(dve, held, ln1_stat, t + 5)
                    nc.vector.bn_aggr(mv1[:], st1[:]).then_inc(ln1_var, 1)
                if there(t - 2):
                    hold(dve, held, ln2_stat, t - 1)
                    nc.vector.bn_aggr(mv2[:], st2[:]).then_inc(ln2_var, 1)
                if there(t):
                    hold(dve, held, top1_in, t + 1)
                    for h in range(H):
                        mx = nc.vector.match_replace(left[:, h], top1[:, h], neg[:, u, h], -BIG)
                    mx.then_inc(left_in, 1)
                if there(t + 1):
                    s, v = t + 1, 1 - u
                    at_least(dve, neg_in, s - 1)
                    at_least(dve, raw_in, s + 1)
                    nc.vector.tensor_reduce(negmin[:, v], raw[:, v], AX.X, ALU.min, negate=True
                                            ).then_inc(min_in, 1)
                if there(t):
                    hold(dve, held, left_in, t + 1)
                    for h in range(H):
                        mx = nc.vector.max(top2[:, h], left[:, h])
                    mx.then_inc(top2_in, 1)
                if there(t - 2):
                    s = t - 2
                    at_least(dve, yT_ps, i - 1)
                    at_least(dve, rstd2, s + 1)
                    nc.vector.tensor_scalar(yhat[:, u:u + 1], xres[:, bass.ds(s, 1), :], mv2[:, 0:1], rs2[:],
                                            ALU.subtract, ALU.mult).then_inc(yhat_in, 1)
                if there(t):
                    at_least(dve, top2_in, t + 1)
                    nc.vector.memset(top2[:, :, DROP - 8:8], -BIG).then_inc(top2_cut, 1)
                if there(t + 4):
                    s = t + 4
                    at_least(dve, xT_ps, s - 1)
                    at_least(dve, rstd1, s + 1)
                    nc.vector.tensor_scalar(xhat[:, u:u + 1], xres[:, bass.ds(s, 1), :], mv1[:, 0:1], rs1[:],
                                            ALU.subtract, ALU.mult).then_inc(xhat_in, 1)
                if there(t - 1):
                    s, v = t - 1, 1 - u
                    cv = c_ps[:, 0:H * (DH + 1)].rearrange("p (h d) -> p h d", d=DH + 1)
                    at_least(dve, ctx_ps, s + 1)
                    nc.vector.reciprocal(rden[:], cv[:, :, DH]).then_inc(rden_in, 1)
                    at_least(dve, ctxT_ps, s - 1)
                    at_least(dve, rden_in, s + 1)
                    nc.vector.tensor_tensor(ctxn[:, v].rearrange("p (h d) -> p h d", d=DH), cv[:, :, 0:DH],
                                            rden[:].rearrange("p (h o) -> p h o", o=1).broadcast_to([P, H, DH]),
                                            ALU.mult).then_inc(ctxn_in, 1)
                if there(t):
                    at_least(dve, probT_ps, 3 * (t - 1))
                    hold(dve, held, top2_cut, t + 1)
                    for h in range(H):
                        mx = nc.vector.match_replace(kept[:, u, h], top2[:, h], left[:, h], -BIG)
                    mx.then_inc(kept_in, 1)

            pipeline(dve, slot, FIRST, LAST + 1, BEGIN, END)


            def finish(n, u):
                k = 2 * n + u
                at_least(dve, stored[u], 16 * n)
                at_least(dve, hT_ps, k + 1)
                nc.vector.scalar_tensor_tensor(fin[:, u, :].rearrange("p (u d) -> p u d", u=2),
                                               pt_ps[u][:].rearrange("p (u d) -> p u d", u=2), tg[:, 1:2],
                                               xres[:, bass.ds(2 * k, 2), :], ALU.mult, ALU.add
                                               ).then_inc(fin_in, 1)

            end_steps(dve, finish)

        @block.scalar
        def _(act):
            act.wait_ge(w_in, 80)
            nc.scalar.activation(tg[:], gcol[:], ACT.Tanh).then_inc(act_set, 1)
            act.wait_ge(dve_set, 2)
            for m in range(KD):
                act.wait_ge(keys_ps, m + 1)
                nc.scalar.activation(keysT[:, m].rearrange("p b n -> p (b n)"), pt_ps[m][:, 0:B * NK],
                                     ACT.Identity, bias=kbias[:, m:m + 1], scale=-0.25).then_inc(keys_sb, 1)
            act.wait_ge(dve_set, 7)
            act.wait_ge(vrow_sb, KC)
            act.wait_ge(kbd_set, KD * B)
            act.wait_ge(pool_set, 9 + KC)

            def exps(i, u, groups):
                s, v, b = 2 * i + u - 1, 1 - u, i // IB if u == 1 else (i - 1) // IB
                at_least(act, ctx_ps, s - 1)
                for g in groups:
                    bank = pt_ps[(u + g) % 2]
                    hold(act, held, probT_ps, 3 * s + g + 1)
                    if g < 2:
                        nc.scalar.activation(probT[:, v, 4 * g:4 * g + 4].rearrange("p c n -> p (c n)"),
                                             bank[:], ACT.Exp, scale=escale[:, bass.ds(b, 1)]
                                             ).then_inc(probT_in, 1)
                    else:
                        nc.scalar.activation(probT[:, v, 8], bank[:, 0:P], ACT.Exp,
                                             scale=escale[:, bass.ds(b, 1)])
                        nc.scalar.activation(probT[0:rows(9), v, 9], bank[0:rows(9), P:2 * P], ACT.Exp,
                                             scale=escale[0:rows(9), bass.ds(b, 1)]).then_inc(probT_in, 1)

            def gate(k, g):
                hold(act, held, gate_ps, 4 * k + g + 1)
                for m in range(KD):
                    src = (g_ps if g < 3 else c_ps)[:, m * 2 * P:(m + 1) * 2 * P]
                    if g < 2:
                        a = nc.scalar.activation(gate_in[:, g, m * 2 * P:(m + 1) * 2 * P], src, ACT.Tanh,
                                                 bias=half[:, 2 + g, m:m + 1], scale=0.5)
                    elif g == 2:
                        a = nc.scalar.activation(gate_in[:, 2, m * 2 * P:(m + 1) * 2 * P], src, ACT.Tanh,
                                                 bias=col[:, 4, m:m + 1])
                    else:
                        a = nc.scalar.activation(hpre[:, bass.ds(k, 1), m * 2 * P:(m + 1) * 2 * P],
                                                 src.rearrange("p (o n) -> p o n", o=1), ACT.Identity,
                                                 bias=col[:, 5, m:m + 1])
                a.then_inc(gate_done, 1)

            def slot(i, u):
                t = 2 * i + u
                k = i - 2
                if there(t - 1):
                    s, v = t - 1, 1 - u
                    at_least(act, kept_in, s + 1)
                    nc.scalar.activation(kept[:, v], kept[:, v], ACT.Abs).then_inc(mag_in, 1)
                if there(t + 1):
                    s, v = t + 1, 1 - u
                    at_least(act, neg_in, s - 1)
                    at_least(act, score_ps, s + 1)
                    flat = raw[:, v].rearrange("p h n -> p (h n)")
                    nc.scalar.activation(flat[:, 0:2 * HB * NK].rearrange("p (a n) -> p a n", a=2),
                                         s_ps[:, 0:2, 0:HB * NK], ACT.Copy)
                    nc.scalar.activation(flat[:, 2 * HB * NK:HK], s_ps[:, 2, 0:HK - 2 * HB * NK],
                                         ACT.Copy).then_inc(raw_in, 1)
                if u == 0 and there(k, IT):
                    at_least(act, gate_ps, 4 * k)
                    at_least(act, yT_ps, k + 1)
                    nc.scalar.activation(yT[:].rearrange("p k u n -> p (k u n)"), pt_ps[0][:], ACT.Copy
                                         ).then_inc(yT_in, 1)
                if there(t + 3):
                    s = t + 3
                    at_least(act, q_ps, i + 1 + u, IT)
                    at_least(act, xT_ps, s + 1)
                    nc.scalar.activation(xT[:, :, 1 - u, :],
                                         pt_ps[1 - u][:, 0:KD * P].rearrange("p (k n) -> p k n", k=KD),
                                         ACT.Copy).then_inc(xT_in, 1)
                if there(t - 1):
                    exps(i, u, (0,))
                if u == 1 and there(k, IT):
                    gate(k, 1)
                if there(t - 1):
                    exps(i, u, (1, 2))
                if u == 0 and there(k, IT):
                    at_least(act, state_in, IB + k)
                    gate(k, 0)
                if u == 1 and there(k, IT):
                    gate(k, 2)
                if there(t - 1):
                    s, v = t - 1, 1 - u
                    at_least(act, attn_ps, s - 1)
                    at_least(act, ctxT_ps, s + 1)
                    nc.scalar.activation(ctxnT[:, v].rearrange("p k n -> p (k n)"), o_ps[:, 0:KD * P],
                                         ACT.Copy).then_inc(ctxT_in, 1)
                if u == 0 and there(i + 1, IT):
                    at_least(act, score_ps, 2 * i + 2)
                    at_least(act, q_ps, i + 2)
                    for m in range(KD):
                        qa = nc.scalar.activation(qT[:, m].rearrange("p u n -> p (u n)"),
                                                  c_ps[:, m * 2 * P:(m + 1) * 2 * P], ACT.Identity,
                                                  bias=col[:, 0, m:m + 1])
                    qa.then_inc(q_in, 1)
                if u == 1 and there(k, IT):
                    gate(k, 3)

            pipeline(act, slot, FIRST, LAST + 1, BEGIN, END)

            act.wait_ge(neg_in, T)
            for j in range(IB):
                act.wait_ge(u_ps, j + 1)
                nc.scalar.activation(ustate_v[:, j], (g_ps if j % 2 else c_ps)[:], ACT.Copy).then_inc(u_in, 1)

            def last_tanh(n, u):
                k = 2 * n + u
                at_least(act, hT_ps, k - 1)
                at_least(act, hsum_in, k + 1)
                nc.scalar.activation(hT[:, u], hsum[:, u], ACT.Tanh).then_inc(h_in, 1)

            end_steps(act, last_tanh)

        @block.tensor
        def _(pe):
            mm = nc.tensor.matmul
            pe.wait_ge(w_in, 80)
            pe.wait_ge(ctx_come, 16)
            for m in range(KD):
                for k in range(KD):
                    last = mm(pt_ps[m][:, 0:B * NK], wa[:, 1, k, m * P:(m + 1) * P], ctx_in[:, k],
                              start=(k == 0), stop=(k == KD - 1))
                last.then_inc(keys_ps, 1)
            for b in range(B):
                if b >= 2:
                    pe.wait_ge(vals_sb, b - 1)
                for k in range(KD):
                    last = mm((c_ps if b % 2 else o_ps)[0:NK, 0:D], ctx_in[:, k, b * NK:(b + 1) * NK],
                              wa[:, 2, k, :], start=(k == 0), stop=(k == KD - 1))
                last.then_inc(vals_ps, 1)
            pe.wait_ge(dve_set, 7)
            pe.wait_ge(vals_sb, B)
            for c in range(KC):
                h0, nh = chunk_heads(c)
                if c >= 2:
                    pe.wait_ge(vrow_sb, c - 1)
                mm((c_ps if c % 2 else o_ps)[0:rows(c), 0:B * nh * DH], sel[:, c * P:c * P + rows(c)],
                   vals[:, :, h0 * DH:(h0 + nh) * DH], start=True, stop=True).then_inc(vrow_ps, 1)
            pe.wait_ge(kbd_set, KD)
            pe.wait_ge(row_set, 2)
            pe.wait_ge(vrow_sb, KC)

            def transposes(s, u, groups):
                for g in groups:
                    at_least(pe, probT_in, 3 * s + (g == 2))
                    for c in range(4 * g, min(4 * g + 4, KC)):
                        last = nc.tensor.transpose(pt_ps[(u + g) % 2][0:rows(c), (c % 4) * P:(c % 4 + 1) * P],
                                                   kept[:, 1 - u].rearrange("p h n -> p (h n)")
                                                   [:, c * P:c * P + rows(c)], ident[:])
                    last.then_inc(probT_ps, 1)

            def gate(k, g, chunks):
                for m in chunks:
                    dst = (g_ps if g < 3 else c_ps)[:, m * 2 * P:(m + 1) * 2 * P]
                    for kk in range(KD):
                        last = mm(dst, wf[:, 2 * g, kk, m * P:(m + 1) * P],
                                  yT[:, kk].rearrange("p u n -> p (u n)"), start=(kk == 0),
                                  stop=(g == 3 and kk == KD - 1))
                    if g < 3:
                        for kk in range(KD):
                            last = mm(dst, wf[:, 2 * g + 1, kk, m * P:(m + 1) * P],
                                      state[:, kk, bass.ds((k % IB) * 2 * P, 2 * P)],
                                      start=False, stop=(kk == KD - 1))
                if chunks[-1] == KD - 1:
                    last.then_inc(gate_ps, 1)

            def slot(i, u):
                t = 2 * i + u
                k = i - 2
                if there(t + 1):
                    s, v, b = t + 1, 1 - u, (i + u) // IB
                    at_least(pe, q_in, i + u + 1)
                    at_least(pe, raw_in, s)
                    if u == 1 and not (isinstance(i, int) and (i + 1) // IB == 0):
                        at_least(pe, kbd_set, KD * B)
                    for a in range(3):
                        n = min(HB, H - HB * a)
                        mm(s_ps[:, a, 0:n * NK], first_row[:],
                           mbias[:, bass.ds(b, 1), :].broadcast_to([P, n, NK]), start=True, stop=True)
                    for h0, h1 in ((0, HB), (HB, HC), (HC, 2 * HB), (2 * HB, H)):
                        m = h0 // HC
                        o = h0 % HB if h0 < 2 * HB else 0
                        last = mm(s_ps[:, h0 // HB, o * NK:(o + h1 - h0) * NK], qT[:, m, v],
                                  kbd[:, bass.ds(b, 1), m, h0 - m * HC:h1 - m * HC, :]
                                  .rearrange("p b h n -> p (b h n)"), start=False, stop=True,
                                  skip_group_check=True)
                    last.then_inc(score_ps, 1)
                if u == 0 and there(k, IT):
                    at_least(pe, yhat_in, 2 * k + 2)
                    at_least(pe, probT_in, 3 * (t - 1), 3 * T)
                    at_least(pe, xT_in, t + 3, T)
                    for uu in range(2):
                        for m in range(KD):
                            last = nc.tensor.transpose(pt_ps[0][:, m * 2 * P + uu * P:m * 2 * P + (uu + 1) * P],
                                                       yhat[:, uu, m * P:(m + 1) * P], ident[:])
                    last.then_inc(yT_ps, 1)
                if there(t + 3):
                    s = t + 3
                    at_least(pe, xhat_in, s + 1)
                    at_least(pe, probT_in, 3 * (t - 1), 3 * T)
                    at_least(pe, yT_in, k + u, IT)
                    at_least(pe, xT_in, s - 1)
                    for m in range(KD):
                        last = nc.tensor.transpose(pt_ps[1 - u][:, m * P:(m + 1) * P],
                                                   xhat[:, 1 - u, m * P:(m + 1) * P], ident[:])
                    last.then_inc(xT_ps, 1)
                if there(t - 1):
                    at_least(pe, mag_in, t)
                    if u == 0:
                        at_least(pe, yT_in, k + 1, IT)
                    transposes(t - 1, u, (0,))
                if there(k, IT):
                    if u == 0:
                        at_least(pe, yT_in, k + 1)
                        at_least(pe, ffn_come, 16)
                        at_least(pe, state_in, k + 1)
                        at_least(pe, gate_done, 4 * k - 1)
                        gate(k, 0, (0,))
                    else:
                        gate(k, 1, (1,))
                if there(t - 1):
                    at_least(pe, xT_in, t + 4, T)
                    transposes(t - 1, u, (1, 2))
                if there(k, IT):
                    if u == 0:
                        gate(k, 0, (1,))
                    else:
                        at_least(pe, gate_done, 4 * k + 2)
                        gate(k, 2, (0,))
                if there(t - 1):
                    s, v = t - 1, 1 - u
                    b = i // IB if u == 1 else (i - 1) // IB
                    at_least(pe, ctxn_in, s)
                    if u == 1:
                        at_least(pe, q_in, i + 2, IT)
                    else:
                        at_least(pe, gate_done, 4 * k)
                    for c in range(KC):
                        h0, nh = chunk_heads(c)
                        if c % 4 == 0:
                            at_least(pe, probT_in, 3 * s + c // 4 + 1)
                        last = mm(c_ps[:, h0 * (DH + 1):(h0 + nh) * (DH + 1)], probT[0:rows(c), v, c],
                                  vbd[0:rows(c), bass.ds(b, 1), c, 0:nh * (DH + 1)]
                                  .rearrange("p b n -> p (b n)"),
                                  start=(c == 0), stop=(c == KC - 1), skip_group_check=True)
                    last.then_inc(ctx_ps, 1)
                if u == 1 and there(k, IT):
                    gate(k, 2, (1,))
                if there(t - 1):
                    s, v = t - 1, 1 - u
                    at_least(pe, x2_in, s)
                    at_least(pe, ctxn_in, s + 1)
                    for m in range(KD):
                        last = nc.tensor.transpose(o_ps[:, m * P:(m + 1) * P], ctxn[:, v, m * P:(m + 1) * P],
                                                   ident[:])
                    last.then_inc(ctxT_ps, 1)
                if u == 0 and there(i + 1, IT):
                    at_least(pe, xT_in, 2 * i + 4)
                    at_least(pe, ctxn_in, t, T)
                    at_least(pe, gate_done, 4 * k)
                    for m in range(KD):
                        for kk in range(KD):
                            last = mm(c_ps[:, m * 2 * P:(m + 1) * 2 * P], wa[:, 0, kk, m * P:(m + 1) * P],
                                      xT[:, kk].rearrange("p u n -> p (u n)"), start=(kk == 0),
                                      stop=(kk == KD - 1))
                    last.then_inc(q_ps, 1)
                if there(k, IT):
                    if u == 0:
                        at_least(pe, gate_done, 4 * k + 1)
                        gate(k, 1, (0,))
                    else:
                        at_least(pe, ctxn_in, t, T)
                        at_least(pe, q_in, i + 2, IT)
                        gate(k, 3, (0, 1))
                if there(t - 1):
                    s, v = t - 1, 1 - u
                    at_least(pe, ctxT_in, s + 1)
                    for m in range(KD):
                        last = mm(o_ps[:, D:2 * D], ctxnT[:, v, m], wa[:, 3, m, :], start=(m == 0),
                                  stop=(m == KD - 1))
                    last.then_inc(attn_ps, 1)

            pipeline(pe, slot, FIRST, LAST + 1, BEGIN, END)

            pe.wait_ge(state_in, IB + IT)
            pe.wait_ge(gate_done, 4 * IT)
            pe.wait_ge(ctxn_in, T)
            for j in range(IB):
                bank = g_ps if j % 2 else c_ps
                if j >= 2:
                    pe.wait_ge(u_in, j - 1)
                for m in range(KD):
                    for kk in range(KD):
                        last = mm(bank[:, m * 2 * P:(m + 1) * 2 * P], wf[:, 7, kk, m * P:(m + 1) * P],
                                  state[:, kk, j * 2 * P:(j + 1) * 2 * P], start=(kk == 0), stop=(kk == KD - 1))
                last.then_inc(u_ps, 1)
            pe.wait_ge(probT_in, 3 * T)

            def turn_back(n, u):
                k = 2 * n + u
                at_least(pe, fin_in, k - 1)
                at_least(pe, h_in, k + 1)
                for uu in range(2):
                    for m in range(KD):
                        last = nc.tensor.transpose(pt_ps[u][:, uu * D + m * P:uu * D + (m + 1) * P],
                                                   hT[:, u, m * 2 * P + uu * P:m * 2 * P + (uu + 1) * P],
                                                   ident[:])
                last.then_inc(hT_ps, 1)

            end_steps(pe, turn_back)


def kernel(**inputs):
    import numpy as _np
    import concourse.bacc as _bacc
    from concourse import mybir as _mybir
    from concourse.bass_utils import run_bass_kernel_spmd as _run

    def get(name):
        return _np.asarray(inputs[name])

    def tr(name):
        return get(name).T

    cols = ["L0_xattn_wq_b", "L0_xattn_wk_b", "L0_ffn_bf", "L0_ffn_bi", "L0_ffn_bc", "L0_ffn_bo", "L0_ffn_in_c"]
    arrays = {
        "x": get("x"),
        "ctxT": get("ctx_1024")[:, ::-1].transpose(2, 0, 1).reshape(256, 4 * 77),
        "mask": _np.broadcast_to(get("mask_BxS2_bf1").view(_np.uint8)[:, ::-1].reshape(1, -1), (128, 4 * 77)),
        "w_attn": _np.stack([tr(f"L0_xattn_w{n}_w") for n in "qkvo"]),
        "w_ffn": _np.stack([tr(f"L0_ffn_{m}{n}") for n in "fico" for m in "wu"]),
        "cols": _np.stack([get(n) for n in cols]).reshape(7, 2, 128).transpose(2, 0, 1).reshape(128, 14),
        "brows": _np.broadcast_to(_np.stack([get("L0_xattn_wv_b"), get("L0_xattn_wo_b")]), (128, 2, 256)),
        "gates": _np.broadcast_to(_np.concatenate([get("g_xattn"), get("g_ffn")]), (128, 2)),
    }
    arrays = {f"{n}_dram": _np.ascontiguousarray(a) for n, a in arrays.items()}
    nc = _bacc.Bacc("TRN2", target_bir_lowering=False, num_devices=1)
    args = [nc.dram_tensor(n, a.shape, _mybir.dt.from_np(a.dtype), kind="ExternalInput").ap()
            for n, a in arrays.items()]
    out = nc.dram_tensor("out_dram", (4, 1024, 256), _mybir.dt.float32, kind="ExternalOutput").ap()
    build(nc, *args, out)
    r = _run(nc, [arrays], core_ids=[0])
    return r.results[0]["out_dram"]
```

```python
from contextlib import ExitStack

import concourse.bass as bass
from concourse import mybir

ALU = mybir.AluOpType
ACT = mybir.ActivationFunctionType
AX = mybir.AxisListType
F32 = mybir.dt.float32
F32R = mybir.dt.float32r
BF16 = mybir.dt.bfloat16
U8 = mybir.dt.uint8

P = 128
B, N, D, H, DH, NK, TOPK = 4, 1024, 256, 16, 16, 77, 64
KD = D // P
T = B * N // P
IT = T // 2
IB = N // (2 * P)
HK = H * NK
DROP = NK - TOPK
HB = 6
HC = P // DH
KC = (HK + P - 1) // P
VW = 3 * (DH + 1)
BIG = 2.0 ** 126
EPS = 1e-5


def chunk_heads(c):
    first = c * P // NK
    return first, (min((c + 1) * P, HK) - 1) // NK - first + 1


def rows(c):
    return min(P, HK - c * P)


def at_least(eng, sem, n, most=None):
    if isinstance(n, int):
        if most is not None:
            n = min(n, most)
        if n <= 0:
            return
    eng.wait_ge(sem, n)


def hold(eng, held, sem, n, most=None):
    if isinstance(n, int):
        at_least(eng, sem, n, most)
        return
    eng.wait_ge(sem, n)
    eng.sem_inc(held, 1)


def pipeline(eng, slot, start, last, begin, end):
    for i in range(start, begin):
        for u in range(2):
            slot(i, u)
    with eng.Fori(begin, end) as i:
        for u in range(2):
            slot(i, u)
    for i in range(end, last):
        for u in range(2):
            slot(i, u)


def final(k):
    return isinstance(k, int) and k == IT - 1


def slot_is(i, n):
    return isinstance(i, int) and i == n


def there(t, n=T):
    return not isinstance(t, int) or 0 <= t < n


FIRST, LAST = -2, IT + 3
BEGIN, END = 3, IT - 2


def build(nc, x, ctxT, mask, w_attn, w_ffn, cols, brows, gates, out):
    x_rows = x.rearrange("b n d -> (b n) d")
    out_rows = out.rearrange("b n d -> (b n) d")
    with ExitStack() as stack:
        def sb(name, shape, dt=F32):
            return stack.enter_context(nc.sbuf_tensor(name, shape, dt))

        def ps(name, shape, dt=F32):
            return stack.enter_context(nc.psum_tensor(name, shape, dt))

        def sem(name):
            return stack.enter_context(nc.semaphore(name))

        xres = sb("xres", [P, T, D])
        hpre = sb("hpre", [P, IT, 2, D])
        state = sb("state", [P, KD, N])
        state_h = sb("state_h", [P, 2, KD, 2 * P], F32R)
        state_l = sb("state_l", [P, 2, KD, 2 * P], F32R)
        kbd = sb("kbd", [P, B, KD, HC, NK])
        vbd = sb("vbd", [P, B, KC, VW])
        wa = sb("wa", [P, 2, KD, D])
        wfh, wfl = sb("wfh", [P, 8, KD, D], F32R), sb("wfl", [P, 8, KD, D], F32R)
        col = sb("col", [P, 7, KD])
        half = sb("half", [P, 7, KD])
        kbias = sb("kbias", [P, KD])
        brow = sb("brow", [P, 3, D])
        gcol = sb("gcol", [P, 2])
        tg = sb("tg", [P, 2])
        tgbo = sb("tgbo", [P, D])
        ident = sb("ident", [P, P])
        mask8 = sb("mask8", [P, B, NK], U8)
        mbias = sb("mbias", [P, B, NK], BF16)
        first_row = sb("first_row", [P, P], BF16)
        anyk = sb("anyk", [P, B])
        escale = sb("escale", [P, B])
        minus_half = sb("minus_half", [P, 1])
        st1, mv1, ve1, rs1 = sb("st1", [P, 6]), sb("mv1", [P, 2]), sb("ve1", [P, 1]), sb("rs1", [P, 1])
        nm1, nm2 = sb("nm1", [P, 1]), sb("nm2", [P, 1])
        st2, mv2, ve2, rs2 = sb("st2", [P, 6]), sb("mv2", [P, 2]), sb("ve2", [P, 1]), sb("rs2", [P, 1])
        xhat = sb("xhat", [P, 2, D])
        xT = sb("xT", [P, KD, 2, P])
        qT = sb("qT", [P, KD, 2, P])
        neg = sb("neg", [P, 2, H, NK])
        kept = sb("kept", [P, 2, H, NK])
        negmin = sb("negmin", [P, 2, H])
        top1 = sb("top1", [P, H, 8])
        top2 = sb("top2", [P, H, 8])
        probT = sb("probT", [P, 2, KC, P])
        rden = sb("rden", [P, H])
        ctxn = sb("ctxn", [P, 2, D])
        ctxnT = sb("ctxnT", [P, 2, KD, P])
        yhat = sb("yhat", [P, 2, D])
        yT = sb("yT", [P, KD, 2, P])
        yTh, yTl = sb("yTh", [P, KD, 2, P], F32R), sb("yTl", [P, KD, 2, P], F32R)
        gate_in = sb("gate_in", [P, 3, KD * 2 * P])
        stage = hpre[:].rearrange("p i u d -> p (i u d)")
        wf = stage[:, 0:8 * KD * D].rearrange("p (a k d) -> p a k d", a=8, k=KD)
        o = 8 * KD * D
        sel = stage[0:NK, o:o + HK]
        o += HK
        hmask = stage[:, o:o + KC * H].rearrange("p (c h) -> p c h", h=H)
        o += KC * H
        cmask = stage[:, o:o + HC]
        o += HC
        ctx_in = stage[:, o:o + KD * B * NK].rearrange("p (k n) -> p k n", k=KD)
        o += KD * B * NK
        wkv = stage[:, o:o + 2 * KD * D].rearrange("p (a k d) -> p a k d", a=2, k=KD)
        keysT = probT[:, 0, 0:5, :].rearrange("p c n -> p (c n)")[:, 0:KD * B * NK]
        keysT = keysT.rearrange("p (m b n) -> p m b n", m=KD, b=B)
        vals = probT[0:NK, 1, 0:8, :].rearrange("p c n -> p (c n)").rearrange("p (b d) -> p b d", b=B)
        ustate = neg[:].rearrange("p u h n -> p (u h n)")[:, 0:IB * 2 * D]
        ustate = ustate.rearrange("p (j u d) -> p j u d", j=IB, u=2)

        s_ps = ps("s_ps", [P, 3, 512])
        pt_ps = [ps(f"pt_ps{n}", [P, 512]) for n in range(2)]
        c_ps = ps("c_ps", [P, 512])
        o_ps = ps("o_ps", [P, 512])
        g_ps = ps("g_ps", [P, 512])

        w_in, ctx_come, wqo_come, ffn_come = sem("w_in"), sem("ctx_come"), sem("wqo_come"), sem("ffn_come")
        x_in, held = sem("x_in"), sem("held")
        row_set = sem("row_set")
        pool_set, dve_set, act_set = sem("pool_set"), sem("dve_set"), sem("act_set")
        keys_ps, keys_sb, kbd_set = sem("keys_ps"), sem("keys_sb"), sem("kbd_set")
        vals_ps, vals_sb = sem("vals_ps"), sem("vals_sb")
        vrow_ps, vrow_sb = sem("vrow_ps"), sem("vrow_sb")
        ln1_stat, ln1_var, ln1_eps, rstd1 = sem("ln1_stat"), sem("ln1_var"), sem("ln1_eps"), sem("rstd1")
        ln2_stat, ln2_var, ln2_eps, rstd2 = sem("ln2_stat"), sem("ln2_var"), sem("ln2_eps"), sem("rstd2")
        rs1_in, rs2_in = sem("rs1_in"), sem("rs2_in")
        xhat_in, xT_ps, xT_in = sem("xhat_in"), sem("xT_ps"), sem("xT_in")
        q_ps, q_in = sem("q_ps"), sem("q_in")
        score_ps, raw_in, neg_in = sem("score_ps"), sem("raw_in"), sem("neg_in")
        min_in, top1_in, left_in, top2_in, top2_cut, kept_in = (
            sem("min_in"), sem("top1_in"), sem("left_in"), sem("top2_in"), sem("top2_cut"), sem("kept_in"))
        mag_in = sem("mag_in")
        probT_ps, probT_in, ctx_ps, rden_in, ctxn_in = (
            sem("probT_ps"), sem("probT_in"), sem("ctx_ps"), sem("rden_in"), sem("ctxn_in"))
        ctxT_ps, ctxT_in, attn_ps, biased, x2_in = (
            sem("ctxT_ps"), sem("ctxT_in"), sem("attn_ps"), sem("biased"), sem("x2_in"))
        yhat_in, yT_ps, yT_in, yTl_in = sem("yhat_in"), sem("yT_ps"), sem("yT_in"), sem("yTl_in")
        f_in, i_in = sem("f_in"), sem("i_in")
        wfh_in, wfl_in, state_h_in, state_l_in = (
            sem("wfh_in"), sem("wfl_in"), sem("state_h_in"), sem("state_l_in"))
        gate_ps, gate_done, old_part, input_part, state_in = (
            sem("gate_ps"), sem("gate_done"), sem("old_part"), sem("input_part"), sem("state_in"))
        u_ps, u_in, sum_in, last_sum_in, h_in, fin_in, stored = (
            sem("u_ps"), sem("u_in"), sem("sum_in"), sem("last_sum_in"), sem("h_in"), sem("fin_in"),
            sem("stored"))

        setup_banks = (o_ps, g_ps, c_ps)

        def gate_bank(k, g):
            return s_ps[:, g] if final(k) else g_ps[:]

        def state_bank(j):
            return o_ps if j % 2 else g_ps

        block = stack.enter_context(nc.Block())

        @block.sync
        def _(sp):
            sp.dma_start(ctx_in, ctxT.rearrange("(k p) n -> p k n", p=P)).then_inc(ctx_come, 16)
            sp.dma_start(wkv, w_attn[0:2].rearrange("a (k p) n -> p a k n", p=P)).then_inc(ctx_come, 16)
            sp.dma_start(col[:], cols.rearrange("p (a k) -> p a k", k=KD)).then_inc(w_in, 16)
            sp.dma_start(gcol[:], gates).then_inc(w_in, 16)

            def load(i):
                sp.dma_start(xres[:, bass.ds(2 * i, 2), :],
                             x_rows[bass.ds(2 * P * i, 2 * P), :].rearrange("(u p) d -> p u d", p=P)
                             ).then_inc(x_in, 16)

            load(0)
            sp.dma_start(mask8[:], mask.rearrange("p (b n) -> p b n", b=B)).then_inc(w_in, 16)
            sp.dma_start(brow[:], brows).then_inc(w_in, 16)
            sp.dma_start(wa[:], w_attn[2:4].rearrange("a (k p) n -> p a k n", p=P)).then_inc(wqo_come, 16)
            sp.wait_ge(x_in, 16)
            load(1)
            sp.dma_start(wf, w_ffn.rearrange("a (k p) n -> p a k n", p=P)).then_inc(ffn_come, 16)
            with sp.Fori(2, IT) as i:
                hold(sp, held, x_in, 16 * i)
                load(i)

            with sp.Fori(0, IB) as j:
                for b in range(B):
                    hold(sp, held, fin_in, B * j + b + 1)
                    sp.dma_start(out_rows[bass.ds(2 * P * (IB * b + j), 2 * P), :]
                                 .rearrange("(u p) d -> p u d", p=P),
                                 xres[:, bass.ds(2 * (IB * b + j), 2), :]).then_inc(stored, 16)
            sp.wait_ge(stored, 16 * IT)

        @block.gpsimd
        def _(pool):
            nc.gpsimd.memset(ident[:], 0.0).then_inc(pool_set, 1)
            nc.gpsimd.memset(cmask, 1.0).then_inc(pool_set, 1)
            nc.gpsimd.memset(hmask, 1.0).then_inc(pool_set, 1)
            nc.gpsimd.memset(minus_half[:], -0.5).then_inc(pool_set, 1)
            nc.gpsimd.memset(first_row[:], 0.0).then_inc(row_set, 1)
            pool.wait_ge(row_set, 1)
            nc.gpsimd.memset(first_row[0:1], 1.0).then_inc(row_set, 1)
            pool.wait_ge(pool_set, 4)
            nc.gpsimd.affine_select(out=ident[:], in_=ident[:], compare_op=ALU.not_equal, fill=1.0, base=0,
                                    pattern=[[-1, P]], channel_multiplier=1).then_inc(pool_set, 1)
            nc.gpsimd.affine_select(out=cmask, in_=cmask, compare_op=ALU.is_ge, fill=0.0, base=0,
                                    pattern=[[-DH, HC]], channel_multiplier=1).then_inc(pool_set, 1)
            nc.gpsimd.affine_select(out=hmask, in_=hmask, compare_op=ALU.is_ge, fill=0.0, base=0,
                                    pattern=[[P, KC], [-NK, H]], channel_multiplier=1).then_inc(pool_set, 1)
            pool.wait_ge(pool_set, 7)
            nc.gpsimd.affine_select(out=cmask, in_=cmask, compare_op=ALU.is_ge, fill=0.0, base=DH - 1,
                                    pattern=[[DH, HC]], channel_multiplier=-1).then_inc(pool_set, 1)
            nc.gpsimd.affine_select(out=hmask, in_=hmask, compare_op=ALU.is_ge, fill=0.0, base=NK - 1,
                                    pattern=[[-P, KC], [NK, H]], channel_multiplier=-1).then_inc(pool_set, 1)
            pool.wait_ge(pool_set, 9)
            for c in range(KC):
                h0, nh = chunk_heads(c)
                ones = vbd[:, :, c, :].rearrange("p b (h d) -> p b h d", d=DH + 1)[:, :, 0:nh, DH]
                nc.gpsimd.tensor_copy(ones, hmask[:, c:c + 1, h0:h0 + nh].broadcast_to([P, B, nh])
                                      ).then_inc(pool_set, 1)
            pool.wait_ge(dve_set, 6)

            def inverse_deviation(t, mv, ve, rs, nm, var_in, eps_in, rs_in, rstd, applied):
                hold(pool, held, var_in, t + 1)
                nc.gpsimd.tensor_scalar(ve[:], mv[:, 1:2], EPS, None, ALU.add).then_inc(eps_in, 1)
                at_least(pool, eps_in, t + 1)
                at_least(pool, applied, t)
                nc.gpsimd.tensor_tensor(rs[:], ve[:], minus_half[:], ALU.pow).then_inc(rs_in, 1)
                hold(pool, held, rs_in, t + 1)
                nc.gpsimd.tensor_scalar(nm[:], mv[:, 0:1], rs[:], -1.0, ALU.mult, ALU.mult).then_inc(rstd, 1)

            def slot(i, u):
                t = 2 * i + u
                k = i - 3
                if u == 0 and there(i - 2, IT):
                    at_least(pool, gate_ps, 4 * (i - 2))
                    hold(pool, held, yT_in, i - 1)
                    nc.gpsimd.tensor_tensor(yTl[:], yT[:], yTh[:].bitcast(F32), ALU.subtract
                                            ).then_inc(yTl_in, 1)
                if there(t + 4):
                    inverse_deviation(t + 4, mv1, ve1, rs1, nm1, ln1_var, ln1_eps, rs1_in, rstd1, xhat_in)
                if there(t - 2):
                    inverse_deviation(t - 2, mv2, ve2, rs2, nm2, ln2_var, ln2_eps, rs2_in, rstd2, yhat_in)
                if u == 0 and there(k, IT):
                    hold(pool, held, gate_done, 4 * k + 3)
                    nc.gpsimd.tensor_scalar(gate_in[:, 1], gate_in[:, 1], 0.5, 0.5, ALU.mult, ALU.add
                                            ).then_inc(i_in, 1)
                    hold(pool, held, i_in, k + 1)
                    nc.gpsimd.tensor_tensor(gate_in[:, 1], gate_in[:, 1], gate_in[:, 2], ALU.mult
                                            ).then_inc(input_part, 1)
                    at_least(pool, state_l_in, k + 1)
                    at_least(pool, old_part, k + 1)
                    hold(pool, held, input_part, k + 1)
                    nc.gpsimd.tensor_tensor(state[:, :, bass.ds((k % IB) * 2 * P, 2 * P)],
                                            gate_in[:, 0].rearrange("p (k n) -> p k n", k=KD),
                                            gate_in[:, 1].rearrange("p (k n) -> p k n", k=KD), ALU.add
                                            ).then_inc(state_in, 1)
                if there(t + 1):
                    s, v = t + 1, 1 - u
                    at_least(pool, min_in, s + 1)
                    nc.gpsimd.tensor_tensor(neg[:, v], neg[:, v],
                                            negmin[:, v].rearrange("p (h o) -> p h o", o=1)
                                            .broadcast_to([P, H, NK]), ALU.add).then_inc(neg_in, 1)
                if there(t + 3):
                    s = t + 3
                    hold(pool, held, xhat_in, s + 1)
                    nc.gpsimd.tensor_tensor(xres[:, bass.ds(s, 1), :], xres[:, bass.ds(s, 1), :],
                                            tgbo[:].rearrange("p (o d) -> p o d", o=1), ALU.add
                                            ).then_inc(biased, 1)
                if u == 0 and there(i - 1, IT):
                    state_low(i - 1)
                if u == 1 and there(i - 2, IT):
                    hold(pool, held, gate_done, 4 * (i - 2) + 1)
                    nc.gpsimd.tensor_scalar(gate_in[:, 0], gate_in[:, 0], 0.5, 0.5, ALU.mult, ALU.add
                                            ).then_inc(f_in, 1)
                    hold(pool, held, f_in, i - 1)
                    nc.gpsimd.tensor_tensor(gate_in[:, 0].rearrange("p (k n) -> p k n", k=KD),
                                            gate_in[:, 0].rearrange("p (k n) -> p k n", k=KD),
                                            state[:, :, bass.ds(((i - 2) % IB) * 2 * P, 2 * P)], ALU.mult
                                            ).then_inc(old_part, 1)
                if u == 1 and slot_is(i, -1):
                    pool.wait_ge(keys_sb, KD)
                    for b in range(1, B):
                        for m in range(KD):
                            nc.gpsimd.tensor_tensor(kbd[:, b, m], keysT[:, m, b:b + 1, :].broadcast_to([P, HC, NK]),
                                                    cmask.rearrange("p (h o) -> p h o", o=1).broadcast_to([P, HC, NK]),
                                                    ALU.mult).then_inc(kbd_set, 1)
                if u == 1 and slot_is(i, 0):
                    for n in range(8):
                        pool.wait_ge(wfh_in, n + 1)
                        nc.gpsimd.tensor_tensor(wfl[:, n], wf[:, n], wfh[:, n].bitcast(F32), ALU.subtract
                                                ).then_inc(wfl_in, 1)
                if u == 1 and slot_is(i, IT + 1):
                    last_sums(0)

            def state_low(k):
                hold(pool, held, state_h_in, k + 1)
                nc.gpsimd.tensor_tensor(state_l[:, bass.ds(k % 2, 1)].rearrange("p o k n -> p (o k) n"),
                                        state[:, :, bass.ds((k % IB) * 2 * P, 2 * P)],
                                        state_h[:, bass.ds(k % 2, 1)].bitcast(F32)
                                        .rearrange("p o k n -> p (o k) n"), ALU.subtract
                                        ).then_inc(state_l_in, 1)

            def last_sums(j):
                pool.wait_ge(u_in, j + 1)
                pool.wait_ge(gate_done, 4 * (IB * (B - 1) + j + 1))
                for b in range(B // 2, B):
                    nc.gpsimd.tensor_tensor(hpre[:, IB * b + j], hpre[:, IB * b + j], ustate[:, j], ALU.add
                                            ).then_inc(last_sum_in, 1)

            pipeline(pool, slot, FIRST, LAST + 1, BEGIN, END)

            for j in range(1, IB):
                last_sums(j)

        @block.vector
        def _(dve):
            dve.wait_ge(w_in, 64)
            nc.vector.tensor_scalar(kbias[:], col[:, 1], -0.25, None, ALU.mult).then_inc(dve_set, 1)
            nc.vector.tensor_scalar(half[:], col[:], 0.5, None, ALU.mult).then_inc(dve_set, 1)
            nc.vector.tensor_scalar(mbias[:], mask8[:], -BIG, BIG, ALU.mult, ALU.add).then_inc(dve_set, 1)
            nc.vector.tensor_reduce(anyk[:], mask8[:], AX.X, ALU.max).then_inc(dve_set, 1)
            dve.wait_ge(dve_set, 4)
            nc.vector.tensor_scalar(escale[:], anyk[:], -1.0, None, ALU.mult).then_inc(dve_set, 1)
            dve.wait_ge(act_set, 1)
            nc.vector.tensor_scalar(tgbo[:], brow[:, 1], tg[:, 0:1], None, ALU.mult).then_inc(dve_set, 1)
            def set_up_keys():
                dve.wait_ge(pool_set, 9)
                dve.wait_ge(keys_sb, KD)
                for m in range(KD):
                    nc.vector.tensor_tensor(kbd[:, 0, m], keysT[:, m, 0:1, :].broadcast_to([P, HC, NK]),
                                            cmask.rearrange("p (h o) -> p h o", o=1).broadcast_to([P, HC, NK]),
                                            ALU.mult).then_inc(kbd_set, 1)

            def set_up_state():
                dve.wait_ge(pool_set, 9)
                nc.vector.tensor_copy(sel.rearrange("k (h n) -> k h n", h=H),
                                      ident[0:NK, 0:NK].rearrange("p (o n) -> p o n", o=1)
                                      .broadcast_to([NK, H, NK])).then_inc(dve_set, 1)
                for j in range(IB):
                    nc.vector.tensor_copy(state[:, :, j * 2 * P:(j + 1) * 2 * P],
                                          col[:, 6, :].rearrange("p (k o) -> p k o", o=1)
                                          .broadcast_to([P, KD, 2 * P])).then_inc(state_in, 1)

                for b in range(0, B, 2):
                    dve.wait_ge(vals_ps, b // 2 + 1)
                    nc.vector.tensor_tensor(vals[:, b:b + 2],
                                            setup_banks[b // 2][0:NK, 0:2 * D].rearrange("p (b d) -> p b d", b=2),
                                            brow[0:NK, 0:1].broadcast_to([NK, 2, D]), ALU.add
                                            ).then_inc(vals_sb, 1)

            def set_up_values(chunks):
                for c in chunks:
                    h0, nh = chunk_heads(c)
                    dve.wait_ge(vrow_ps, c + 1)
                    v_out = vbd[0:rows(c), :, c, :].rearrange("p b (h d) -> p b h d", d=DH + 1)[:, :, 0:nh, 0:DH]
                    v_in = setup_banks[c % 3][0:rows(c), 0:B * nh * DH]
                    nc.vector.tensor_tensor(v_out, v_in.rearrange("p (b h d) -> p b h d", b=B, d=DH),
                                            hmask[0:rows(c), c:c + 1, h0:h0 + nh].rearrange("p o (h d) -> p o h d", d=1)
                                            .broadcast_to([rows(c), B, nh, DH]), ALU.mult).then_inc(vrow_sb, 1)

            def slot(i, u):
                t = 2 * i + u
                if there(t):
                    hold(dve, held, neg_in, t + 1)
                    for h in range(H):
                        mx = nc.vector.max(top1[:, h], neg[:, u, h])
                    mx.then_inc(top1_in, 1)
                if there(t - 2):
                    s = t - 2
                    at_least(dve, biased, s + 1)
                    at_least(dve, attn_ps, s + 1)
                    nc.vector.scalar_tensor_tensor(xres[:, bass.ds(s, 1), :],
                                                   o_ps[:, D:2 * D].rearrange("p (o d) -> p o d", o=1),
                                                   tg[:, 0:1], xres[:, bass.ds(s, 1), :], ALU.mult, ALU.add
                                                   ).then_inc(x2_in, 1)
                if there(t + 4):
                    s = t + 4
                    hold(dve, held, x_in, 16 * (i + 3))
                    hold(dve, held, rstd1, s)
                    nc.vector.bn_stats(st1[:], xres[:, bass.ds(s, 1), :]).then_inc(ln1_stat, 1)
                if there(t - 2):
                    s = t - 2
                    hold(dve, held, x2_in, s + 1)
                    hold(dve, held, rstd2, s)
                    nc.vector.bn_stats(st2[:], xres[:, bass.ds(s, 1), :]).then_inc(ln2_stat, 1)
                if there(t + 4):
                    hold(dve, held, ln1_stat, t + 5)
                    nc.vector.bn_aggr(mv1[:], st1[:]).then_inc(ln1_var, 1)
                if there(t - 2):
                    hold(dve, held, ln2_stat, t - 1)
                    nc.vector.bn_aggr(mv2[:], st2[:]).then_inc(ln2_var, 1)
                if there(t):
                    hold(dve, held, top1_in, t + 1)
                    for h in range(H):
                        mx = nc.vector.match_replace(neg[:, u, h], top1[:, h], neg[:, u, h], -BIG)
                    mx.then_inc(left_in, 1)
                if u == 1 and slot_is(i, -1):
                    set_up_values(range(3))
                if there(t + 1):
                    s, v = t + 1, 1 - u
                    at_least(dve, raw_in, s + 1)
                    nc.vector.tensor_reduce(negmin[:, v], neg[:, v], AX.X, ALU.min, negate=True
                                            ).then_inc(min_in, 1)
                if slot_is(i, -2) and u == 1:
                    set_up_keys()
                if u == 0 and slot_is(i, -1):
                    set_up_state()
                if u == 1 and slot_is(i, -1):
                    set_up_values(range(3, KC))
                if there(t):
                    hold(dve, held, left_in, t + 1)
                    for h in range(H):
                        mx = nc.vector.max(top2[:, h], neg[:, u, h])
                    mx.then_inc(top2_in, 1)
                if there(t):
                    at_least(dve, top2_in, t + 1)
                    nc.vector.memset(top2[:, :, DROP - 8:8], -BIG).then_inc(top2_cut, 1)
                if there(t - 1):
                    s, v = t - 1, 1 - u
                    cv = c_ps[:, 0:H * (DH + 1)].rearrange("p (h d) -> p h d", d=DH + 1)
                    at_least(dve, ctx_ps, s + 1)
                    nc.vector.reciprocal(rden[:], cv[:, :, DH]).then_inc(rden_in, 1)
                    at_least(dve, ctxT_ps, s - 1)
                    at_least(dve, rden_in, s + 1)
                    nc.vector.tensor_tensor(ctxn[:, v].rearrange("p (h d) -> p h d", d=DH), cv[:, :, 0:DH],
                                            rden[:].rearrange("p (h o) -> p h o", o=1).broadcast_to([P, H, DH]),
                                            ALU.mult).then_inc(ctxn_in, 1)
                if there(t):
                    at_least(dve, probT_ps, 3 * (t - 1))
                    hold(dve, held, top2_cut, t + 1)
                    for h in range(H):
                        mx = nc.vector.match_replace(kept[:, u, h], top2[:, h], neg[:, u, h], -BIG)
                    mx.then_inc(kept_in, 1)
                if slot_is(i, IT + 1):
                    if u == 0:
                        state_low(0)
                        sums(0)
                    else:
                        state_low(1)
                        state_low(2)
                        finish(0)

            def state_low(j):
                k = IT + j
                dve.wait_ge(state_l_in, k)
                dve.wait_ge(state_h_in, k + 1)
                nc.vector.tensor_tensor(state_l[:, k % 2], state[:, :, j * 2 * P:(j + 1) * 2 * P],
                                        state_h[:, k % 2].bitcast(F32), ALU.subtract).then_inc(state_l_in, 1)

            def sums(j):
                dve.wait_ge(u_ps, j + 1)
                dve.wait_ge(kept_in, T)
                nc.vector.tensor_tensor(ustate[:, j], state_bank(j)[:].rearrange("p (u d) -> p u d", u=2),
                                        brow[:, 2:3].broadcast_to([P, 2, D]), ALU.add).then_inc(u_in, 1)
                dve.wait_ge(u_in, j + 1)
                dve.wait_ge(gate_done, 4 * (IB * (B - 1) + j + 1))
                for b in range(B // 2):
                    nc.vector.tensor_tensor(hpre[:, IB * b + j], hpre[:, IB * b + j], ustate[:, j], ALU.add
                                            ).then_inc(sum_in, 1)

            def finish(j):
                for b in range(B):
                    k = IB * b + j
                    dve.wait_ge(h_in, B * j + b + 1)
                    nc.vector.scalar_tensor_tensor(xres[:, 2 * k:2 * k + 2], hpre[:, k], tg[:, 1:2],
                                                   xres[:, 2 * k:2 * k + 2], ALU.mult, ALU.add
                                                   ).then_inc(fin_in, 1)

            pipeline(dve, slot, FIRST, LAST + 1, BEGIN, END)

            sums(1)
            state_low(3)
            sums(2)
            finish(1)
            sums(3)
            finish(2)
            finish(3)

        @block.scalar
        def _(act):
            act.wait_ge(w_in, 64)
            nc.scalar.activation(tg[:], gcol[:], ACT.Tanh).then_inc(act_set, 1)
            act.wait_ge(dve_set, 2)
            for m in range(KD):
                act.wait_ge(keys_ps, m + 1)
                nc.scalar.activation(keysT[:, m].rearrange("p b n -> p (b n)"), pt_ps[m][:, 0:B * NK],
                                     ACT.Identity, bias=kbias[:, m:m + 1], scale=-0.25).then_inc(keys_sb, 1)
            def exps(i, u, groups):
                s, v, b = 2 * i + u - 1, 1 - u, i // IB if u == 1 else (i - 1) // IB
                at_least(act, ctx_ps, s - 1)
                for g in groups:
                    bank = pt_ps[(u + g) % 2]
                    hold(act, held, probT_ps, 3 * s + g + 1)
                    if g < 2:
                        nc.scalar.activation(probT[:, v, 4 * g:4 * g + 4].rearrange("p c n -> p (c n)"),
                                             bank[:], ACT.Exp, scale=escale[:, bass.ds(b, 1)]
                                             ).then_inc(probT_in, 1)
                    else:
                        nc.scalar.activation(probT[:, v, 8], bank[:, 0:P], ACT.Exp,
                                             scale=escale[:, bass.ds(b, 1)])
                        nc.scalar.activation(probT[0:rows(9), v, 9], bank[0:rows(9), P:2 * P], ACT.Exp,
                                             scale=escale[0:rows(9), bass.ds(b, 1)]).then_inc(probT_in, 1)

            def gate(k, g):
                hold(act, held, gate_ps, 4 * k + g + 1)
                if g == 3:
                    nc.scalar.activation(hpre[:, bass.ds(k, 1)].rearrange("p o u d -> p (o u d)"), c_ps[:],
                                         ACT.Copy).then_inc(gate_done, 1)
                    return
                for m in range(KD):
                    src = gate_bank(k, g)[:, m * 2 * P:(m + 1) * 2 * P]
                    if g < 2:
                        a = nc.scalar.activation(gate_in[:, g, m * 2 * P:(m + 1) * 2 * P], src, ACT.Tanh,
                                                 bias=half[:, 2 + g, m:m + 1], scale=0.5)
                    else:
                        a = nc.scalar.activation(gate_in[:, 2, m * 2 * P:(m + 1) * 2 * P], src, ACT.Tanh,
                                                 bias=col[:, 4, m:m + 1])
                a.then_inc(gate_done, 1)

            def state_high(k):
                hold(act, held, state_in, k + 1)
                hold(act, held, gate_ps, 4 * (k - 2) + 3)
                nc.scalar.activation(state_h[:, bass.ds(k % 2, 1)].rearrange("p o k n -> p (o k) n"),
                                     state[:, :, bass.ds((k % IB) * 2 * P, 2 * P)], ACT.Copy
                                     ).then_inc(state_h_in, 1)

            def tanhs(j):
                for b in range(B):
                    if b < B // 2:
                        act.wait_ge(sum_in, B // 2 * j + b + 1)
                    else:
                        act.wait_ge(last_sum_in, B // 2 * (j - 1) + b + 1)
                    nc.scalar.activation(hpre[:, IB * b + j], hpre[:, IB * b + j], ACT.Tanh).then_inc(h_in, 1)

            def slot(i, u):
                t = 2 * i + u
                k = i - 2
                if there(t - 1):
                    s, v = t - 1, 1 - u
                    at_least(act, kept_in, s + 1)
                    nc.scalar.activation(kept[:, v], kept[:, v], ACT.Abs).then_inc(mag_in, 1)
                if u == 0 and there(k, IT):
                    at_least(act, gate_ps, 4 * k)
                    at_least(act, yT_ps, k + 1)
                    nc.scalar.activation(yTh[:].rearrange("p k u n -> p (k u n)"), pt_ps[0][:], ACT.Copy)
                    nc.scalar.activation(yT[:].rearrange("p k u n -> p (k u n)"), pt_ps[0][:], ACT.Copy
                                         ).then_inc(yT_in, 1)
                if there(t + 3):
                    s = t + 3
                    at_least(act, q_ps, i + 1 + u, IT)
                    at_least(act, xT_ps, s + 1)
                    nc.scalar.activation(xT[:, :, 1 - u, :],
                                         pt_ps[1 - u][:, 0:KD * P].rearrange("p (k n) -> p k n", k=KD),
                                         ACT.Copy).then_inc(xT_in, 1)
                if there(t + 1):
                    s, v = t + 1, 1 - u
                    at_least(act, kept_in, s - 1)
                    at_least(act, score_ps, s + 1)
                    flat = neg[:, v].rearrange("p h n -> p (h n)")
                    nc.scalar.activation(flat[:, 0:2 * HB * NK].rearrange("p (a n) -> p a n", a=2),
                                         s_ps[:, 0:2, 0:HB * NK], ACT.Copy)
                    nc.scalar.activation(flat[:, 2 * HB * NK:HK], s_ps[:, 2, 0:HK - 2 * HB * NK],
                                         ACT.Copy).then_inc(raw_in, 1)
                if u == 0 and there(i - 1, IT + 1):
                    state_high(i - 1)
                if u == 1 and slot_is(i, 0):
                    act.wait_ge(dve_set, 7)
                    act.wait_ge(vrow_sb, KC)
                    act.wait_ge(kbd_set, KD * B)
                    act.wait_ge(pool_set, 9 + KC)
                if there(t - 1):
                    exps(i, u, (0,))
                if u == 1 and there(k, IT):
                    gate(k, 1)
                if there(t - 1):
                    exps(i, u, (1, 2))
                if there(t + 4):
                    s = t + 4
                    at_least(act, xT_ps, s - 1)
                    hold(act, held, rstd1, s + 1)
                    nc.scalar.activation(xhat[:, u:u + 1], xres[:, bass.ds(s, 1), :], ACT.Identity,
                                         bias=nm1[:], scale=rs1[:]).then_inc(xhat_in, 1)
                if there(t - 2):
                    s = t - 2
                    at_least(act, yT_ps, i - 1)
                    hold(act, held, rstd2, s + 1)
                    nc.scalar.activation(yhat[:, u:u + 1], xres[:, bass.ds(s, 1), :], ACT.Identity,
                                         bias=nm2[:], scale=rs2[:]).then_inc(yhat_in, 1)
                if u == 0 and there(k, IT):
                    at_least(act, state_in, IB + k)
                    gate(k, 0)
                if u == 1 and there(k, IT):
                    gate(k, 2)
                if there(t - 1):
                    s, v = t - 1, 1 - u
                    at_least(act, attn_ps, s - 1)
                    at_least(act, ctxT_ps, s + 1)
                    nc.scalar.activation(ctxnT[:, v].rearrange("p k n -> p (k n)"), o_ps[:, 0:KD * P],
                                         ACT.Copy).then_inc(ctxT_in, 1)
                if u == 0 and there(i + 1, IT):
                    at_least(act, score_ps, 2 * i + 2)
                    at_least(act, q_ps, i + 2)
                    for m in range(KD):
                        qa = nc.scalar.activation(qT[:, m].rearrange("p u n -> p (u n)"),
                                                  c_ps[:, m * 2 * P:(m + 1) * 2 * P], ACT.Identity,
                                                  bias=col[:, 0, m:m + 1])
                    qa.then_inc(q_in, 1)
                if u == 1 and there(k, IT):
                    at_least(act, wfl_in, 8)
                    gate(k, 3)
                if u == 0 and slot_is(i, 0):
                    act.wait_ge(ffn_come, 16)
                    for n in range(8):
                        nc.scalar.activation(wfh[:, n], wf[:, n], ACT.Copy).then_inc(wfh_in, 1)
                if u == 1 and slot_is(i, IT + 1):
                    state_high(IT + 1)
                    last_high(2)
                    tanhs(0)

            def last_high(j):
                act.wait_ge(state_in, IT + j + 1)
                act.wait_ge(u_ps, j - 1)
                nc.scalar.activation(state_h[:, j % 2], state[:, :, j * 2 * P:(j + 1) * 2 * P], ACT.Copy
                                     ).then_inc(state_h_in, 1)

            pipeline(act, slot, FIRST, LAST + 1, BEGIN, END)

            last_high(3)
            for j in range(1, IB):
                tanhs(j)

        @block.tensor
        def _(pe):
            mm = nc.tensor.matmul
            pe.wait_ge(ctx_come, 32)
            for m in range(KD):
                for k in range(KD):
                    last = mm(pt_ps[m][:, 0:B * NK], wkv[:, 0, k, m * P:(m + 1) * P], ctx_in[:, k],
                              start=(k == 0), stop=(k == KD - 1))
                last.then_inc(keys_ps, 1)
            for b in range(B):
                for k in range(KD):
                    last = mm(setup_banks[b // 2][0:NK, b % 2 * D:(b % 2 + 1) * D],
                              ctx_in[:, k, b * NK:(b + 1) * NK], wkv[:, 1, k, :],
                              start=(k == 0), stop=(k == KD - 1))
                if b % 2:
                    last.then_inc(vals_ps, 1)
            pe.wait_ge(keys_sb, KD)
            pe.wait_ge(pool_set, 9)
            pe.wait_ge(row_set, 2)

            def set_up_values():
                pe.wait_ge(dve_set, 7)
                pe.wait_ge(vals_sb, B // 2)
                for c in range(KC):
                    h0, nh = chunk_heads(c)
                    if c >= 3:
                        pe.wait_ge(vrow_sb, c - 2)
                    mm(setup_banks[c % 3][0:rows(c), 0:B * nh * DH], sel[:, c * P:c * P + rows(c)],
                       vals[:, :, h0 * DH:(h0 + nh) * DH], start=True, stop=True).then_inc(vrow_ps, 1)

            def transposes(s, u, groups):
                for g in groups:
                    at_least(pe, probT_in, 3 * s + (g == 2))
                    for c in range(4 * g, min(4 * g + 4, KC)):
                        last = nc.tensor.transpose(pt_ps[(u + g) % 2][0:rows(c), (c % 4) * P:(c % 4 + 1) * P],
                                                   kept[:, 1 - u].rearrange("p h n -> p (h n)")
                                                   [:, c * P:c * P + rows(c)], ident[:])
                    last.then_inc(probT_ps, 1)

            def gate(k, g, chunks):
                for m in chunks:
                    cols_m = slice(m * P, (m + 1) * P)

                    def of_state(w, part):
                        return [(w[:, 2 * g + 1, kk, cols_m],
                                 part[:, bass.ds(k % 2, 1), kk].rearrange("p o n -> p (o n)")) for kk in range(KD)]

                    def of_input(w, part):
                        return [(w[:, 2 * g, kk, cols_m], part[:, kk].rearrange("p u n -> p (u n)"))
                                for kk in range(KD)]

                    dst = gate_bank(k, g)[:, m * 2 * P:(m + 1) * 2 * P]
                    products(dst, of_state(wfh, state_h) + of_state(wfh, state_l) + of_state(wfl, state_h)
                             + of_input(wfh, yTh) + of_input(wfl, yTh), stop=False)
                    if g == 0 and m == 0:
                        at_least(pe, yTl_in, k + 1)
                    done = products(dst, of_input(wfh, yTl), start=False)
                if chunks[-1] == KD - 1:
                    done.then_inc(gate_ps, 1)

            def products(dst, terms, start=True, stop=True):
                for n, (a, b) in enumerate(terms):
                    last = mm(dst, a, b, start=start and n == 0, stop=stop and n == len(terms) - 1)
                return last

            def out_input():
                for uu in range(2):
                    last = products(c_ps[:, uu * D:(uu + 1) * D],
                                    [(part[:, kk, uu], w[:, 6, kk, :]) for kk in range(KD)
                                     for w, part in ((wfh, yTh), (wfh, yTl), (wfl, yTh))])
                last.then_inc(gate_ps, 1)

            def out_state(j):
                pe.wait_ge(state_l_in, IT + j + 1)
                if j == 0:
                    pe.wait_ge(gate_done, 4 * (IT - 2) + 3)
                elif j == 1:
                    pe.wait_ge(x2_in, T)
                at_least(pe, u_in, j - 1)
                for uu in range(2):
                    last = products(state_bank(j)[:, uu * D:(uu + 1) * D],
                                    [(part[:, j % 2, kk, uu * P:(uu + 1) * P], w[:, 7, kk, :]) for kk in range(KD)
                                     for w, part in ((wfh, state_h), (wfh, state_l), (wfl, state_h))])
                last.then_inc(u_ps, 1)

            def slot(i, u):
                t = 2 * i + u
                k = i - 2
                if u == 0 and there(k, IT):
                    at_least(pe, yhat_in, 2 * k + 2)
                    at_least(pe, probT_in, 3 * (t - 1), 3 * T)
                    at_least(pe, xT_in, t + 3, T)
                    for uu in range(2):
                        for m in range(KD):
                            last = nc.tensor.transpose(pt_ps[0][:, m * 2 * P + uu * P:m * 2 * P + (uu + 1) * P],
                                                       yhat[:, uu, m * P:(m + 1) * P], ident[:])
                    last.then_inc(yT_ps, 1)
                if there(t + 3):
                    s = t + 3
                    at_least(pe, xhat_in, s + 1)
                    at_least(pe, probT_in, 3 * (t - 1), 3 * T)
                    at_least(pe, yT_in, k + u, IT)
                    at_least(pe, xT_in, s - 1)
                    for m in range(KD):
                        last = nc.tensor.transpose(pt_ps[1 - u][:, m * P:(m + 1) * P],
                                                   xhat[:, 1 - u, m * P:(m + 1) * P], ident[:])
                    last.then_inc(xT_ps, 1)
                if there(t + 1):
                    s, v, b = t + 1, 1 - u, (i + u) // IB
                    at_least(pe, q_in, i + u + 1)
                    at_least(pe, raw_in, s)
                    if slot_is(i, -1):
                        pe.wait_ge(kbd_set, KD)
                        pe.wait_ge(dve_set, 5)
                    if u == 1 and not (isinstance(i, int) and (i + 1) // IB == 0):
                        at_least(pe, kbd_set, KD * B)
                    for a in range(3):
                        n = min(HB, H - HB * a)
                        mm(s_ps[:, a, 0:n * NK], first_row[:],
                           mbias[:, bass.ds(b, 1), :].broadcast_to([P, n, NK]), start=True, stop=True)
                    for h0, h1 in ((0, HB), (HB, HC), (HC, 2 * HB), (2 * HB, H)):
                        m = h0 // HC
                        o = h0 % HB if h0 < 2 * HB else 0
                        last = mm(s_ps[:, h0 // HB, o * NK:(o + h1 - h0) * NK], qT[:, m, v],
                                  kbd[:, bass.ds(b, 1), m, h0 - m * HC:h1 - m * HC, :]
                                  .rearrange("p b h n -> p (b h n)"), start=False, stop=True,
                                  skip_group_check=True)
                    last.then_inc(score_ps, 1)
                if u == 1 and slot_is(i, -1):
                    set_up_values()
                if there(t - 1):
                    at_least(pe, mag_in, t)
                    if u == 0:
                        at_least(pe, yT_in, k + 1, IT)
                    transposes(t - 1, u, (0,))
                if there(k, IT):
                    if u == 0:
                        at_least(pe, yT_in, k + 1)
                        at_least(pe, wfl_in, 8)
                        at_least(pe, state_l_in, k + 1)
                        if final(k):
                            pe.wait_ge(raw_in, T)
                        else:
                            at_least(pe, gate_done, 4 * k - 1)
                        gate(k, 0, (0,))
                    else:
                        if not final(k):
                            at_least(pe, gate_done, 4 * k + 1)
                        gate(k, 1, (0, 1))
                if there(t - 1):
                    at_least(pe, xT_in, t + 4, T)
                    transposes(t - 1, u, (1, 2))
                if there(t - 1):
                    s, v = t - 1, 1 - u
                    b = i // IB if u == 1 else (i - 1) // IB
                    at_least(pe, ctxn_in, s)
                    if u == 1:
                        at_least(pe, q_in, i + 2, IT)
                    else:
                        at_least(pe, gate_done, 4 * k)
                    for c in range(KC):
                        h0, nh = chunk_heads(c)
                        if c % 4 == 0:
                            at_least(pe, probT_in, 3 * s + c // 4 + 1)
                        last = mm(c_ps[:, h0 * (DH + 1):(h0 + nh) * (DH + 1)], probT[0:rows(c), v, c],
                                  vbd[0:rows(c), bass.ds(b, 1), c, 0:nh * (DH + 1)]
                                  .rearrange("p b n -> p (b n)"),
                                  start=(c == 0), stop=(c == KC - 1), skip_group_check=True)
                    last.then_inc(ctx_ps, 1)
                if there(k, IT):
                    if u == 0:
                        gate(k, 0, (1,))
                    else:
                        if not final(k):
                            at_least(pe, gate_done, 4 * k + 2)
                        gate(k, 2, (0, 1))
                if there(t - 1):
                    s, v = t - 1, 1 - u
                    at_least(pe, x2_in, s)
                    at_least(pe, ctxn_in, s + 1)
                    for m in range(KD):
                        last = nc.tensor.transpose(o_ps[:, m * P:(m + 1) * P], ctxn[:, v, m * P:(m + 1) * P],
                                                   ident[:])
                    last.then_inc(ctxT_ps, 1)
                if u == 0 and there(i + 1, IT):
                    at_least(pe, xT_in, 2 * i + 4)
                    at_least(pe, ctxn_in, t, T)
                    at_least(pe, gate_done, 4 * k)
                    if slot_is(i, -1):
                        pe.wait_ge(wqo_come, 16)
                    if slot_is(i, 0):
                        pe.wait_ge(vrow_sb, KC)
                    for m in range(KD):
                        for kk in range(KD):
                            last = mm(c_ps[:, m * 2 * P:(m + 1) * 2 * P], wa[:, 0, kk, m * P:(m + 1) * P],
                                      xT[:, kk].rearrange("p u n -> p (u n)"), start=(kk == 0),
                                      stop=(kk == KD - 1))
                    last.then_inc(q_ps, 1)
                if u == 1 and there(k, IT):
                    at_least(pe, ctxn_in, t, T)
                    at_least(pe, q_in, i + 2, IT)
                    out_input()
                if there(t - 1):
                    s, v = t - 1, 1 - u
                    at_least(pe, ctxT_in, s + 1)
                    for m in range(KD):
                        last = mm(o_ps[:, D:2 * D], ctxnT[:, v, m], wa[:, 1, m, :], start=(m == 0),
                                  stop=(m == KD - 1))
                    last.then_inc(attn_ps, 1)
                if slot_is(i, IT + 1):
                    out_state(u)

            pipeline(pe, slot, FIRST, LAST + 1, BEGIN, END)

            out_state(2)
            out_state(3)


def kernel(**inputs):
    import numpy as _np
    import concourse.bacc as _bacc
    from concourse import mybir as _mybir
    from concourse.bass_utils import run_bass_kernel_spmd as _run

    def get(name):
        return _np.asarray(inputs[name])

    def tr(name):
        return get(name).T

    cols = ["L0_xattn_wq_b", "L0_xattn_wk_b", "L0_ffn_bf", "L0_ffn_bi", "L0_ffn_bc", "L0_ffn_bo", "L0_ffn_in_c"]
    arrays = {
        "x": get("x"),
        "ctxT": get("ctx_1024")[:, ::-1].transpose(2, 0, 1).reshape(256, 4 * 77),
        "mask": _np.broadcast_to(get("mask_BxS2_bf1").view(_np.uint8)[:, ::-1].reshape(1, -1), (128, 4 * 77)),
        "w_attn": _np.stack([tr(f"L0_xattn_w{n}_w") for n in "kvqo"]),
        "w_ffn": _np.stack([tr(f"L0_ffn_{m}{n}") for n in "fico" for m in "wu"]),
        "cols": _np.stack([get(n) for n in cols]).reshape(7, 2, 128).transpose(2, 0, 1).reshape(128, 14),
        "brows": _np.broadcast_to(_np.stack([get("L0_xattn_wv_b"), get("L0_xattn_wo_b"), get("L0_ffn_bo")]), (128, 3, 256)),
        "gates": _np.broadcast_to(_np.concatenate([get("g_xattn"), get("g_ffn")]), (128, 2)),
    }
    arrays = {f"{n}_dram": _np.ascontiguousarray(a) for n, a in arrays.items()}
    nc = _bacc.Bacc("TRN2", target_bir_lowering=False, num_devices=1)
    args = [nc.dram_tensor(n, a.shape, _mybir.dt.from_np(a.dtype), kind="ExternalInput").ap()
            for n, a in arrays.items()]
    out = nc.dram_tensor("out_dram", (4, 1024, 256), _mybir.dt.float32, kind="ExternalOutput").ap()
    build(nc, *args, out)
    r = _run(nc, [arrays], core_ids=[0])
    return r.results[0]["out_dram"]
```

```python
from contextlib import ExitStack

import concourse.bass as bass
from concourse import mybir

ALU = mybir.AluOpType
ACT = mybir.ActivationFunctionType
AX = mybir.AxisListType
F32 = mybir.dt.float32
F32R = mybir.dt.float32r
BF16 = mybir.dt.bfloat16
U8 = mybir.dt.uint8

P = 128
B, N, D, H, DH, NK, TOPK = 4, 1024, 256, 16, 16, 77, 64
KD = D // P
T = B * N // P
IT = T // 2
IB = N // (2 * P)
HK = H * NK
DROP = NK - TOPK
HB = 6
HC = P // DH
KC = (HK + P - 1) // P
VW = 3 * (DH + 1)
BIG = 2.0 ** 126
EPS = 1e-5


def chunk_heads(c):
    first = c * P // NK
    return first, (min((c + 1) * P, HK) - 1) // NK - first + 1


def rows(c):
    return min(P, HK - c * P)


def at_least(eng, sem, n, most=None):
    if isinstance(n, int):
        if most is not None:
            n = min(n, most)
        if n <= 0:
            return
    eng.wait_ge(sem, n)


def hold(eng, held, sem, n, most=None):
    if isinstance(n, int):
        at_least(eng, sem, n, most)
        return
    eng.wait_ge(sem, n)
    eng.sem_inc(held, 1)


def pipeline(eng, slot, start, last, begin, end):
    for i in range(start, begin):
        for u in range(2):
            slot(i, u)
    with eng.Fori(begin, end) as i:
        for u in range(2):
            slot(i, u)
    for i in range(end, last):
        for u in range(2):
            slot(i, u)


def own_banks(k):
    return isinstance(k, int) and k == IT - 2


def slot_is(i, n):
    return isinstance(i, int) and i == n


FIRST_HEADS = 12
PART = (2, 2, 0, 1)
SHARE = (4, 3, 1, 1)


def there(t, n=T):
    return not isinstance(t, int) or 0 <= t < n


FIRST, LAST = -3, IT + 1
BEGIN, END = 3, IT - 3


def build(nc, x, ctxT, mask, w_attn, w_ffn, cols, brows, gates, out):
    x_rows = x.rearrange("b n d -> (b n) d")
    out_rows = out.rearrange("b n d -> (b n) d")
    with ExitStack() as stack:
        def sb(name, shape, dt=F32):
            return stack.enter_context(nc.sbuf_tensor(name, shape, dt))

        def ps(name, shape, dt=F32):
            return stack.enter_context(nc.psum_tensor(name, shape, dt))

        def sem(name):
            return stack.enter_context(nc.semaphore(name))

        xres = sb("xres", [P, T, D])
        hpre = sb("hpre", [P, IT, 2, D])
        state = sb("state", [P, KD, N])
        state_h = sb("state_h", [P, 3, KD, 2 * P], F32R)
        state_l = sb("state_l", [P, 3, KD, 2 * P], F32R)
        kbd = sb("kbd", [P, B, KD, HC, NK])
        vbd = sb("vbd", [P, B, KC, VW])
        wa = sb("wa", [P, 2, KD, D])
        wfh, wfl = sb("wfh", [P, 8, KD, D], F32R), sb("wfl", [P, 8, KD, D], F32R)
        col = sb("col", [P, 7, KD])
        half = sb("half", [P, 7, KD])
        kbias = sb("kbias", [P, KD])
        brow = sb("brow", [P, 3, D])
        gcol = sb("gcol", [P, 2])
        tg = sb("tg", [P, 2])
        tgbo = sb("tgbo", [P, D])
        ident = sb("ident", [P, P])
        mbias = sb("mbias", [P, B, NK], BF16)
        first_row = sb("first_row", [P, P], BF16)
        anyk = sb("anyk", [P, B])
        escale = sb("escale", [P, B])
        minus_half = sb("minus_half", [P, 1])
        st1, mv1, ve1, rs1 = sb("st1", [P, 6]), sb("mv1", [P, 2]), sb("ve1", [P, 1]), sb("rs1", [P, 1])
        nm1, nm2 = sb("nm1", [P, 1]), sb("nm2", [P, 1])
        st2, mv2, ve2, rs2 = sb("st2", [P, 6]), sb("mv2", [P, 2]), sb("ve2", [P, 1]), sb("rs2", [P, 1])
        xhat = sb("xhat", [P, 2, D])
        xT = sb("xT", [P, KD, 2, P])
        qT = sb("qT", [P, KD, 2, P])
        neg = sb("neg", [P, 2, H, NK])
        kept = sb("kept", [P, 2, H, NK])
        negmin = sb("negmin", [P, 2, H])
        top1 = sb("top1", [P, H, 8])
        top2 = sb("top2", [P, H, 8])
        probT = sb("probT", [P, 2, KC, P])
        rden = sb("rden", [P, H])
        ctxn = sb("ctxn", [P, 2, D])
        ctxnT = sb("ctxnT", [P, 2, KD, P])
        yhat = sb("yhat", [P, 2, D])
        yT = sb("yT", [P, KD, 2, P])
        yTh, yTl = sb("yTh", [P, KD, 2, P], F32R), sb("yTl", [P, KD, 2, P], F32R)
        gate_in = sb("gate_in", [P, 3, KD * 2 * P])
        stage = hpre[:].rearrange("p i u d -> p (i u d)")
        wf = stage[:, 0:8 * KD * D].rearrange("p (a k d) -> p a k d", a=8, k=KD)
        o = 8 * KD * D
        sel = stage[0:NK, o:o + HK]
        o += HK
        hmask = stage[:, o:o + KC * H].rearrange("p (c h) -> p c h", h=H)
        o += KC * H
        cmask = stage[:, o:o + HC]
        o += HC
        ctx_in = stage[:, o:o + KD * B * NK].rearrange("p (k n) -> p k n", k=KD)
        o += KD * B * NK
        wkv = stage[:, o:o + 2 * KD * D].rearrange("p (a k d) -> p a k d", a=2, k=KD)
        o += 2 * KD * D
        mask8 = stage[:, o:o + B * NK // 4].bitcast(U8).rearrange("p (b n) -> p b n", b=B)
        keysT = probT[:, 0, 0:5, :].rearrange("p c n -> p (c n)")[:, 0:KD * B * NK]
        keysT = keysT.rearrange("p (m b n) -> p m b n", m=KD, b=B)
        vals = probT[0:NK, 1, 0:8, :].rearrange("p c n -> p (c n)").rearrange("p (b d) -> p b d", b=B)
        ustate = neg[:].rearrange("p u h n -> p (u h n)")[:, 0:IB * 2 * D]
        ustate = ustate.rearrange("p (j u d) -> p j u d", j=IB, u=2)

        s_ps = ps("s_ps", [P, 3, 512])
        pt_ps = [ps(f"pt_ps{n}", [P, 512]) for n in range(2)]
        c_ps = ps("c_ps", [P, 512])
        o_ps = ps("o_ps", [P, 512])
        g_ps = ps("g_ps", [P, 512])

        w_in, ctx_come, wqo_come, ffn_come = sem("w_in"), sem("ctx_come"), sem("wqo_come"), sem("ffn_come")
        x_in, held = sem("x_in"), sem("held")
        row_set = sem("row_set")
        pool_set, dve_set, act_set = sem("pool_set"), sem("dve_set"), sem("act_set")
        keys_ps, keys_sb, kbd_set = sem("keys_ps"), sem("keys_sb"), sem("kbd_set")
        vals_ps, vals_sb = sem("vals_ps"), sem("vals_sb")
        vrow_ps, vrow_sb = sem("vrow_ps"), sem("vrow_sb")
        ln1_stat, ln1_var, ln1_eps, rstd1 = sem("ln1_stat"), sem("ln1_var"), sem("ln1_eps"), sem("rstd1")
        ln2_stat, ln2_var, ln2_eps, rstd2 = sem("ln2_stat"), sem("ln2_var"), sem("ln2_eps"), sem("rstd2")
        rs1_in, rs2_in, last_parts = sem("rs1_in"), sem("rs2_in"), sem("last_parts")
        last_h_in, last_l_in = sem("last_h_in"), sem("last_l_in")
        xhat_in, xT_ps, xT_in = sem("xhat_in"), sem("xT_ps"), sem("xT_in")
        q_ps, q_in = sem("q_ps"), sem("q_in")
        score_ps, raw_in, neg_in = sem("score_ps"), sem("raw_in"), sem("neg_in")
        min_in, top1_in, left_in, top2_in, top2_cut, kept_in = (
            sem("min_in"), sem("top1_in"), sem("left_in"), sem("top2_in"), sem("top2_cut"), sem("kept_in"))
        mag_in = sem("mag_in")
        probT_ps, probT_in, ctx_ps, rden_in, ctxn_in = (
            sem("probT_ps"), sem("probT_in"), sem("ctx_ps"), sem("rden_in"), sem("ctxn_in"))
        ctxT_ps, ctxT_in, attn_ps, biased, x2_in = (
            sem("ctxT_ps"), sem("ctxT_in"), sem("attn_ps"), sem("biased"), sem("x2_in"))
        yhat_in, yT_ps, yT_in, yTl_in = sem("yhat_in"), sem("yT_ps"), sem("yT_in"), sem("yTl_in")
        f_in, i_in = sem("f_in"), sem("i_in")
        wfh_in, wfl_in, state_h_in, state_l_in = (
            sem("wfh_in"), sem("wfl_in"), sem("state_h_in"), sem("state_l_in"))
        gate_ps, gate_done, old_part, input_part, state_in = (
            sem("gate_ps"), sem("gate_done"), sem("old_part"), sem("input_part"), sem("state_in"))
        u_ps, u_in, sum_in, last_sum_in, h_in, fin_in, stored = (
            sem("u_ps"), sem("u_in"), sem("sum_in"), sem("last_sum_in"), sem("h_in"), sem("fin_in"),
            sem("stored"))

        setup_banks = (o_ps, g_ps, c_ps)

        def gate_bank(k, g):
            if own_banks(k):
                return s_ps[:, g]
            if isinstance(k, int) and k == IT - 1:
                return (g_ps[:], pt_ps[1][:], s_ps[:, 0])[g]
            return g_ps[:]

        def state_bank(j):
            return (g_ps[:], o_ps[:], s_ps[:, 2], s_ps[:, 1])[j]

        block = stack.enter_context(nc.Block())

        @block.sync
        def _(sp):
            sp.dma_start(ctx_in, ctxT.rearrange("(k p) n -> p k n", p=P)).then_inc(ctx_come, 16)
            sp.dma_start(wkv, w_attn[0:2].rearrange("a (k p) n -> p a k n", p=P)).then_inc(ctx_come, 16)
            sp.dma_start(col[:], cols.rearrange("p (a k) -> p a k", k=KD)).then_inc(w_in, 16)
            sp.dma_start(gcol[:], gates).then_inc(w_in, 16)

            def load(i):
                sp.dma_start(xres[:, bass.ds(2 * i, 2), :],
                             x_rows[bass.ds(2 * P * i, 2 * P), :].rearrange("(u p) d -> p u d", p=P)
                             ).then_inc(x_in, 16)

            load(0)
            sp.dma_start(mask8, mask.rearrange("p (b n) -> p b n", b=B)).then_inc(w_in, 16)
            sp.dma_start(brow[:], brows).then_inc(w_in, 16)
            sp.dma_start(wa[:], w_attn[2:4].rearrange("a (k p) n -> p a k n", p=P)).then_inc(wqo_come, 16)
            sp.wait_ge(x_in, 16)
            load(1)
            sp.dma_start(wf, w_ffn.rearrange("a (k p) n -> p a k n", p=P)).then_inc(ffn_come, 16)
            with sp.Fori(2, IT) as i:
                hold(sp, held, x_in, 16 * i)
                load(i)

            with sp.Fori(0, IB) as j:
                for b in range(B):
                    hold(sp, held, fin_in, B * j + b + 1)
                    sp.dma_start(out_rows[bass.ds(2 * P * (IB * b + j), 2 * P), :]
                                 .rearrange("(u p) d -> p u d", p=P),
                                 xres[:, bass.ds(2 * (IB * b + j), 2), :]).then_inc(stored, 16)
            sp.wait_ge(stored, 16 * IT)

        @block.gpsimd
        def _(pool):
            nc.gpsimd.memset(ident[:], 0.0).then_inc(pool_set, 1)
            nc.gpsimd.memset(cmask, 1.0).then_inc(pool_set, 1)
            nc.gpsimd.memset(hmask, 1.0).then_inc(pool_set, 1)
            nc.gpsimd.memset(minus_half[:], -0.5).then_inc(pool_set, 1)
            nc.gpsimd.memset(first_row[:], 0.0).then_inc(row_set, 1)
            pool.wait_ge(row_set, 1)
            nc.gpsimd.memset(first_row[0:1], 1.0).then_inc(row_set, 1)
            pool.wait_ge(pool_set, 4)
            nc.gpsimd.affine_select(out=ident[:], in_=ident[:], compare_op=ALU.not_equal, fill=1.0, base=0,
                                    pattern=[[-1, P]], channel_multiplier=1).then_inc(pool_set, 1)
            nc.gpsimd.affine_select(out=cmask, in_=cmask, compare_op=ALU.is_ge, fill=0.0, base=0,
                                    pattern=[[-DH, HC]], channel_multiplier=1).then_inc(pool_set, 1)
            nc.gpsimd.affine_select(out=hmask, in_=hmask, compare_op=ALU.is_ge, fill=0.0, base=0,
                                    pattern=[[P, KC], [-NK, H]], channel_multiplier=1).then_inc(pool_set, 1)
            pool.wait_ge(pool_set, 7)
            nc.gpsimd.affine_select(out=cmask, in_=cmask, compare_op=ALU.is_ge, fill=0.0, base=DH - 1,
                                    pattern=[[DH, HC]], channel_multiplier=-1).then_inc(pool_set, 1)
            nc.gpsimd.affine_select(out=hmask, in_=hmask, compare_op=ALU.is_ge, fill=0.0, base=NK - 1,
                                    pattern=[[-P, KC], [NK, H]], channel_multiplier=-1).then_inc(pool_set, 1)
            pool.wait_ge(pool_set, 9)
            for c in range(KC):
                h0, nh = chunk_heads(c)
                ones = vbd[:, :, c, :].rearrange("p b (h d) -> p b h d", d=DH + 1)[:, :, 0:nh, DH]
                nc.gpsimd.tensor_copy(ones, hmask[:, c:c + 1, h0:h0 + nh].broadcast_to([P, B, nh])
                                      ).then_inc(pool_set, 1)
            pool.wait_ge(dve_set, 6)

            def inverse_deviation(t, mv, ve, rs, nm, var_in, eps_in, rs_in, rstd, applied):
                hold(pool, held, var_in, t + 1)
                nc.gpsimd.tensor_scalar(ve[:], mv[:, 1:2], EPS, None, ALU.add).then_inc(eps_in, 1)
                at_least(pool, eps_in, t + 1)
                at_least(pool, applied, t)
                nc.gpsimd.tensor_tensor(rs[:], ve[:], minus_half[:], ALU.pow).then_inc(rs_in, 1)
                hold(pool, held, rs_in, t + 1)
                nc.gpsimd.tensor_scalar(nm[:], mv[:, 0:1], rs[:], -1.0, ALU.mult, ALU.mult).then_inc(rstd, 1)

            def slot(i, u):
                t = 2 * i + u
                k = i - 3
                if u == 0 and there(k, IT):
                    new_state(k)
                if u == 0 and there(i - 2, IT):
                    at_least(pool, gate_ps, 4 * (i - 2))
                    hold(pool, held, yT_in, i - 1)
                    nc.gpsimd.tensor_tensor(yTl[:], yT[:], yTh[:].bitcast(F32), ALU.subtract
                                            ).then_inc(yTl_in, 1)
                if there(t + 4):
                    inverse_deviation(t + 4, mv1, ve1, rs1, nm1, ln1_var, ln1_eps, rs1_in, rstd1, xhat_in)
                if there(t - 2):
                    inverse_deviation(t - 2, mv2, ve2, rs2, nm2, ln2_var, ln2_eps, rs2_in, rstd2, yhat_in)
                if there(t + 1):
                    s, v = t + 1, 1 - u
                    at_least(pool, min_in, s + 1)
                    nc.gpsimd.tensor_tensor(neg[:, v], neg[:, v],
                                            negmin[:, v].rearrange("p (h o) -> p h o", o=1)
                                            .broadcast_to([P, H, NK]), ALU.add).then_inc(neg_in, 1)
                if there(t + 3):
                    s = t + 3
                    hold(pool, held, xhat_in, s + 1)
                    nc.gpsimd.tensor_tensor(xres[:, bass.ds(s, 1), :], xres[:, bass.ds(s, 1), :],
                                            tgbo[:].rearrange("p (o d) -> p o d", o=1), ALU.add
                                            ).then_inc(biased, 1)
                if u == 0 and there(i - 1, IT):
                    state_low(i - 1)
                if u == 1 and there(i - 2, IT):
                    old_part_of(i - 2)
                if u == 1 and slot_is(i, -1):
                    pool.wait_ge(keys_sb, KD)
                    for b in range(1, B):
                        for m in range(KD):
                            nc.gpsimd.tensor_tensor(kbd[:, b, m], keysT[:, m, b:b + 1, :].broadcast_to([P, HC, NK]),
                                                    cmask.rearrange("p (h o) -> p h o", o=1).broadcast_to([P, HC, NK]),
                                                    ALU.mult).then_inc(kbd_set, 1)
                if u == 1 and slot_is(i, 0):
                    for n in range(8):
                        pool.wait_ge(wfh_in, n + 1)
                        nc.gpsimd.tensor_tensor(wfl[:, n], wf[:, n], wfh[:, n].bitcast(F32), ALU.subtract
                                                ).then_inc(wfl_in, 1)

            def input_gate(k):
                hold(pool, held, gate_done, 4 * k + 2)
                nc.gpsimd.tensor_scalar(gate_in[:, 1], gate_in[:, 1], 0.5, 0.5, ALU.mult, ALU.add
                                        ).then_inc(i_in, 1)

            def new_state(k):
                input_gate(k)
                hold(pool, held, gate_done, 4 * k + 3)
                hold(pool, held, i_in, k + 1)
                nc.gpsimd.tensor_tensor(gate_in[:, 1], gate_in[:, 1], gate_in[:, 2], ALU.mult
                                        ).then_inc(input_part, 1)
                at_least(pool, state_l_in, k + 1)
                at_least(pool, old_part, k + 1)
                hold(pool, held, input_part, k + 1)
                nc.gpsimd.tensor_tensor(state[:, :, bass.ds((k % IB) * 2 * P, 2 * P)],
                                        gate_in[:, 0].rearrange("p (k n) -> p k n", k=KD),
                                        gate_in[:, 1].rearrange("p (k n) -> p k n", k=KD), ALU.add
                                        ).then_inc(state_in, 1)

            def old_part_of(k):
                hold(pool, held, gate_done, 4 * (k) + 1)
                nc.gpsimd.tensor_scalar(gate_in[:, 0], gate_in[:, 0], 0.5, 0.5, ALU.mult, ALU.add
                                        ).then_inc(f_in, 1)
                hold(pool, held, f_in, k + 1)
                nc.gpsimd.tensor_tensor(gate_in[:, 0].rearrange("p (k n) -> p k n", k=KD),
                                        gate_in[:, 0].rearrange("p (k n) -> p k n", k=KD),
                                        state[:, :, bass.ds(((k) % IB) * 2 * P, 2 * P)], ALU.mult
                                        ).then_inc(old_part, 1)

            def state_low(k):
                hold(pool, held, state_h_in, k + 1)
                nc.gpsimd.tensor_tensor(state_l[:, bass.ds(k % 2, 1)].rearrange("p o k n -> p (o k) n"),
                                        state[:, :, bass.ds((k % IB) * 2 * P, 2 * P)],
                                        state_h[:, bass.ds(k % 2, 1)].bitcast(F32)
                                        .rearrange("p o k n -> p (o k) n"), ALU.subtract
                                        ).then_inc(state_l_in, 1)

            def last_sums(j):
                pool.wait_ge(u_in, j + 1)
                pool.wait_ge(gate_done, 4 * (IB * (B - 1) + j + 1))
                for b in range(SHARE[j], B):
                    nc.gpsimd.tensor_tensor(hpre[:, IB * b + j], hpre[:, IB * b + j], ustate[:, j], ALU.add
                                            ).then_inc(last_sum_in, 1)

            pipeline(pool, slot, FIRST, LAST, BEGIN, END)

            new_state(IT - 2)
            last_sums(1)
            old_part_of(IT - 1)
            input_gate(IT - 1)
            for j in range(2, IB):
                last_sums(j)

        @block.vector
        def _(dve):
            dve.wait_ge(w_in, 64)
            nc.vector.tensor_scalar(kbias[:], col[:, 1], -0.25, None, ALU.mult).then_inc(dve_set, 1)
            nc.vector.tensor_scalar(half[:], col[:], 0.5, None, ALU.mult).then_inc(dve_set, 1)
            nc.vector.tensor_scalar(mbias[:], mask8, -BIG, BIG, ALU.mult, ALU.add).then_inc(dve_set, 1)
            nc.vector.tensor_reduce(anyk[:], mask8, AX.X, ALU.max).then_inc(dve_set, 1)
            dve.wait_ge(dve_set, 4)
            nc.vector.tensor_scalar(escale[:], anyk[:], -1.0, None, ALU.mult).then_inc(dve_set, 1)
            dve.wait_ge(act_set, 1)
            nc.vector.tensor_scalar(tgbo[:], brow[:, 1], tg[:, 0:1], None, ALU.mult).then_inc(dve_set, 1)
            def set_up_keys():
                dve.wait_ge(pool_set, 9)
                dve.wait_ge(keys_sb, KD)
                for m in range(KD):
                    nc.vector.tensor_tensor(kbd[:, 0, m], keysT[:, m, 0:1, :].broadcast_to([P, HC, NK]),
                                            cmask.rearrange("p (h o) -> p h o", o=1).broadcast_to([P, HC, NK]),
                                            ALU.mult).then_inc(kbd_set, 1)

            def set_up_state():
                dve.wait_ge(pool_set, 9)
                nc.vector.tensor_copy(sel.rearrange("k (h n) -> k h n", h=H),
                                      ident[0:NK, 0:NK].rearrange("p (o n) -> p o n", o=1)
                                      .broadcast_to([NK, H, NK])).then_inc(dve_set, 1)
                for j in range(IB):
                    nc.vector.tensor_copy(state[:, :, j * 2 * P:(j + 1) * 2 * P],
                                          col[:, 6, :].rearrange("p (k o) -> p k o", o=1)
                                          .broadcast_to([P, KD, 2 * P])).then_inc(state_in, 1)

                for b in range(0, B, 2):
                    dve.wait_ge(vals_ps, b // 2 + 1)
                    nc.vector.tensor_tensor(vals[:, b:b + 2],
                                            setup_banks[b // 2][0:NK, 0:2 * D].rearrange("p (b d) -> p b d", b=2),
                                            brow[0:NK, 0:1].broadcast_to([NK, 2, D]), ALU.add
                                            ).then_inc(vals_sb, 1)

            def set_up_values(chunks):
                for c in chunks:
                    h0, nh = chunk_heads(c)
                    dve.wait_ge(vrow_ps, c + 1)
                    v_out = vbd[0:rows(c), :, c, :].rearrange("p b (h d) -> p b h d", d=DH + 1)[:, :, 0:nh, 0:DH]
                    v_in = setup_banks[c % 3][0:rows(c), 0:B * nh * DH]
                    nc.vector.tensor_tensor(v_out, v_in.rearrange("p (b h d) -> p b h d", b=B, d=DH),
                                            hmask[0:rows(c), c:c + 1, h0:h0 + nh].rearrange("p o (h d) -> p o h d", d=1)
                                            .broadcast_to([rows(c), B, nh, DH]), ALU.mult).then_inc(vrow_sb, 1)

            def largest(top, u, heads):
                for h in heads:
                    done = nc.vector.max(top[:, h], neg[:, u, h])
                return done

            def take_out(dst, top, u, heads):
                for h in heads:
                    done = nc.vector.match_replace(dst[:, u, h], top[:, h], neg[:, u, h], -BIG)
                return done

            def slot(i, u):
                t = 2 * i + u
                if u == 0 and slot_is(i, IT):
                    state_low(0)
                if there(t):
                    hold(dve, held, neg_in, t + 1)
                    largest(top1, u, range(FIRST_HEADS))
                if there(t - 2):
                    s = t - 2
                    at_least(dve, biased, s + 1)
                    at_least(dve, attn_ps, s + 1)
                    nc.vector.scalar_tensor_tensor(xres[:, bass.ds(s, 1), :],
                                                   o_ps[:, D:2 * D].rearrange("p (o d) -> p o d", o=1),
                                                   tg[:, 0:1], xres[:, bass.ds(s, 1), :], ALU.mult, ALU.add
                                                   ).then_inc(x2_in, 1)
                if there(t):
                    largest(top1, u, range(FIRST_HEADS, H)).then_inc(top1_in, 1)
                if there(t - 2):
                    s = t - 2
                    hold(dve, held, x2_in, s + 1)
                    hold(dve, held, rstd2, s)
                    nc.vector.bn_stats(st2[:], xres[:, bass.ds(s, 1), :]).then_inc(ln2_stat, 1)
                if there(t):
                    hold(dve, held, top1_in, t + 1)
                    take_out(neg, top1, u, range(H - FIRST_HEADS))
                if there(t - 2):
                    hold(dve, held, ln2_stat, t - 1)
                    nc.vector.bn_aggr(mv2[:], st2[:]).then_inc(ln2_var, 1)
                if there(t):
                    take_out(neg, top1, u, range(H - FIRST_HEADS, H)).then_inc(left_in, 1)
                if u == 1 and slot_is(i, -1):
                    set_up_values(range(3))
                if there(t + 1):
                    s, v = t + 1, 1 - u
                    at_least(dve, raw_in, s + 1)
                    nc.vector.tensor_reduce(negmin[:, v], neg[:, v], AX.X, ALU.min, negate=True
                                            ).then_inc(min_in, 1)
                if slot_is(i, -2) and u == 1:
                    set_up_keys()
                if u == 0 and slot_is(i, -1):
                    set_up_state()
                if u == 1 and slot_is(i, -1):
                    set_up_values(range(3, KC))
                if there(t):
                    hold(dve, held, left_in, t + 1)
                    largest(top2, u, range(H)).then_inc(top2_in, 1)
                if u == 0 and slot_is(i, IT):
                    sums(0)
                cv = c_ps[:, 0:H * (DH + 1)].rearrange("p (h d) -> p h d", d=DH + 1)
                if there(t - 1):
                    at_least(dve, ctx_ps, t)
                    nc.vector.reciprocal(rden[:], cv[:, :, DH]).then_inc(rden_in, 1)
                if there(t + 5):
                    s = t + 5
                    hold(dve, held, x_in, 16 * (i + 3 + u))
                    hold(dve, held, rstd1, s)
                    nc.vector.bn_stats(st1[:], xres[:, bass.ds(s, 1), :]).then_inc(ln1_stat, 1)
                if there(t):
                    at_least(dve, top2_in, t + 1)
                    nc.vector.memset(top2[:, :, DROP - 8:8], -BIG).then_inc(top2_cut, 1)
                if there(t - 1):
                    s, v = t - 1, 1 - u
                    at_least(dve, ctxT_ps, s - 1)
                    at_least(dve, rden_in, s + 1)
                    nc.vector.tensor_tensor(ctxn[:, v].rearrange("p (h d) -> p h d", d=DH), cv[:, :, 0:DH],
                                            rden[:].rearrange("p (h o) -> p h o", o=1).broadcast_to([P, H, DH]),
                                            ALU.mult).then_inc(ctxn_in, 1)
                if there(t + 5):
                    hold(dve, held, ln1_stat, t + 6)
                    nc.vector.bn_aggr(mv1[:], st1[:]).then_inc(ln1_var, 1)
                if there(t):
                    at_least(dve, probT_ps, 3 * (t - 1))
                    hold(dve, held, top2_cut, t + 1)
                    take_out(kept, top2, u, range(H)).then_inc(kept_in, 1)
                if u == 1 and slot_is(i, IT):
                    finish(0)

            def state_low(j):
                dve.wait_ge(last_h_in, j + 1)
                nc.vector.tensor_tensor(state_l[:, PART[j]], state[:, :, j * 2 * P:(j + 1) * 2 * P],
                                        state_h[:, PART[j]].bitcast(F32), ALU.subtract).then_inc(last_l_in, 1)

            def sums(j):
                dve.wait_ge(u_ps, j + 1)
                dve.wait_ge(kept_in, T)
                nc.vector.tensor_tensor(ustate[:, j], state_bank(j).rearrange("p (u d) -> p u d", u=2),
                                        brow[:, 2:3].broadcast_to([P, 2, D]), ALU.add).then_inc(u_in, 1)
                dve.wait_ge(u_in, j + 1)
                dve.wait_ge(gate_done, 4 * (IB * (B - 1) + j + 1))
                for b in range(SHARE[j]):
                    nc.vector.tensor_tensor(hpre[:, IB * b + j], hpre[:, IB * b + j], ustate[:, j], ALU.add
                                            ).then_inc(sum_in, 1)

            def finish(j):
                for b in range(B):
                    k = IB * b + j
                    dve.wait_ge(h_in, B * j + b + 1)
                    nc.vector.scalar_tensor_tensor(xres[:, 2 * k:2 * k + 2], hpre[:, k], tg[:, 1:2],
                                                   xres[:, 2 * k:2 * k + 2], ALU.mult, ALU.add
                                                   ).then_inc(fin_in, 1)

            pipeline(dve, slot, FIRST, LAST, BEGIN, END)

            state_low(1)
            dve.wait_ge(yT_in, IT)
            nc.vector.tensor_tensor(yTl[:].rearrange("p k u n -> p (k u n)"), pt_ps[0][:],
                                    yTh[:].rearrange("p k u n -> p (k u n)").bitcast(F32), ALU.subtract
                                    ).then_inc(yTl_in, 1)
            sums(1)
            state_low(2)
            finish(1)
            dve.wait_ge(gate_done, 4 * IT - 1)
            dve.wait_ge(i_in, IT)
            nc.vector.tensor_tensor(gate_in[:, 1], gate_in[:, 1], gate_in[:, 2], ALU.mult).then_inc(input_part, 1)
            dve.wait_ge(old_part, IT)
            dve.wait_ge(input_part, IT)
            nc.vector.tensor_tensor(state[:, :, N - 2 * P:N], gate_in[:, 0].rearrange("p (k n) -> p k n", k=KD),
                                    gate_in[:, 1].rearrange("p (k n) -> p k n", k=KD), ALU.add
                                    ).then_inc(state_in, 1)
            state_low(3)
            sums(2)
            sums(3)
            finish(2)
            finish(3)

        @block.scalar
        def _(act):
            act.wait_ge(w_in, 64)
            nc.scalar.activation(tg[:], gcol[:], ACT.Tanh).then_inc(act_set, 1)
            act.wait_ge(dve_set, 2)
            for m in range(KD):
                act.wait_ge(keys_ps, m + 1)
                nc.scalar.activation(keysT[:, m].rearrange("p b n -> p (b n)"), pt_ps[m][:, 0:B * NK],
                                     ACT.Identity, bias=kbias[:, m:m + 1], scale=-0.25).then_inc(keys_sb, 1)
            def exps(i, u, groups):
                s, v, b = 2 * i + u - 1, 1 - u, i // IB if u == 1 else (i - 1) // IB
                at_least(act, ctx_ps, s - 1)
                for g in groups:
                    bank = pt_ps[(u + g) % 2]
                    hold(act, held, probT_ps, 3 * s + g + 1)
                    if g < 2:
                        nc.scalar.activation(probT[:, v, 4 * g:4 * g + 4].rearrange("p c n -> p (c n)"),
                                             bank[:], ACT.Exp, scale=escale[:, bass.ds(b, 1)]
                                             ).then_inc(probT_in, 1)
                    else:
                        nc.scalar.activation(probT[:, v, 8], bank[:, 0:P], ACT.Exp,
                                             scale=escale[:, bass.ds(b, 1)])
                        nc.scalar.activation(probT[0:rows(9), v, 9], bank[0:rows(9), P:2 * P], ACT.Exp,
                                             scale=escale[0:rows(9), bass.ds(b, 1)]).then_inc(probT_in, 1)

            def gate(k, g):
                hold(act, held, gate_ps, 4 * k + g + 1)
                if g == 3:
                    nc.scalar.activation(hpre[:, bass.ds(k, 1)].rearrange("p o u d -> p (o u d)"), c_ps[:],
                                         ACT.Copy).then_inc(gate_done, 1)
                    return
                for m in range(KD):
                    src = gate_bank(k, g)[:, m * 2 * P:(m + 1) * 2 * P]
                    if g < 2:
                        a = nc.scalar.activation(gate_in[:, g, m * 2 * P:(m + 1) * 2 * P], src, ACT.Tanh,
                                                 bias=half[:, 2 + g, m:m + 1], scale=0.5)
                    else:
                        a = nc.scalar.activation(gate_in[:, 2, m * 2 * P:(m + 1) * 2 * P], src, ACT.Tanh,
                                                 bias=col[:, 4, m:m + 1])
                a.then_inc(gate_done, 1)

            def state_high(k):
                hold(act, held, state_in, k + 1)
                hold(act, held, gate_ps, 4 * (k - 2) + 3)
                nc.scalar.activation(state_h[:, bass.ds(k % 2, 1)].rearrange("p o k n -> p (o k) n"),
                                     state[:, :, bass.ds((k % IB) * 2 * P, 2 * P)], ACT.Copy
                                     ).then_inc(state_h_in, 1)

            def tanhs(j):
                for b in range(B):
                    if b < SHARE[j]:
                        act.wait_ge(sum_in, sum(SHARE[:j]) + b + 1)
                    else:
                        act.wait_ge(last_sum_in, B * j - sum(SHARE[:j + 1]) + b + 1)
                    nc.scalar.activation(hpre[:, IB * b + j], hpre[:, IB * b + j], ACT.Tanh).then_inc(h_in, 1)

            def slot(i, u):
                t = 2 * i + u
                k = i - 2
                if there(t - 1):
                    s, v = t - 1, 1 - u
                    at_least(act, kept_in, s + 1)
                    nc.scalar.activation(kept[:, v], kept[:, v], ACT.Abs).then_inc(mag_in, 1)
                if u == 0 and there(k - 1, IT):
                    at_least(act, wfl_in, 8)
                    gate(k - 1, 3)
                if u == 0 and there(k, IT):
                    at_least(act, gate_ps, 4 * k)
                    at_least(act, yT_ps, k + 1)
                    nc.scalar.activation(yTh[:].rearrange("p k u n -> p (k u n)"), pt_ps[0][:], ACT.Copy)
                    nc.scalar.activation(yT[:].rearrange("p k u n -> p (k u n)"), pt_ps[0][:], ACT.Copy
                                         ).then_inc(yT_in, 1)
                if u == 1 and there(t + 3):
                    s = t + 3
                    at_least(act, q_ps, i + 2, IT)
                    at_least(act, xT_ps, s + 1)
                    nc.scalar.activation(xT[:, :, 0, :],
                                         pt_ps[0][:, 0:KD * P].rearrange("p (k n) -> p k n", k=KD),
                                         ACT.Copy).then_inc(xT_in, 1)
                if there(t + 1):
                    s, v = t + 1, 1 - u
                    at_least(act, kept_in, s - 1)
                    at_least(act, score_ps, s + 1)
                    flat = neg[:, v].rearrange("p h n -> p (h n)")
                    nc.scalar.activation(flat[:, 0:2 * HB * NK].rearrange("p (a n) -> p a n", a=2),
                                         s_ps[:, 0:2, 0:HB * NK], ACT.Copy)
                    nc.scalar.activation(flat[:, 2 * HB * NK:HK], s_ps[:, 2, 0:HK - 2 * HB * NK],
                                         ACT.Copy).then_inc(raw_in, 1)
                if u == 0 and there(t + 3):
                    s = t + 3
                    at_least(act, q_ps, i + 1, IT)
                    at_least(act, xT_ps, s + 1)
                    nc.scalar.activation(xT[:, :, 1, :],
                                         pt_ps[1][:, 0:KD * P].rearrange("p (k n) -> p k n", k=KD),
                                         ACT.Copy).then_inc(xT_in, 1)
                if u == 1 and slot_is(i, 0):
                    act.wait_ge(dve_set, 7)
                    act.wait_ge(vrow_sb, KC)
                    act.wait_ge(kbd_set, KD * B)
                    act.wait_ge(pool_set, 9 + KC)
                if there(t - 1):
                    exps(i, u, (0,))
                if there(t - 1):
                    exps(i, u, (1, 2))
                if u == 1 and there(k, IT):
                    gate(k, 1)
                if there(t + 4):
                    s = t + 4
                    at_least(act, xT_ps, s - 1)
                    hold(act, held, rstd1, s + 1)
                    nc.scalar.activation(xhat[:, u:u + 1], xres[:, bass.ds(s, 1), :], ACT.Identity,
                                         bias=nm1[:], scale=rs1[:]).then_inc(xhat_in, 1)
                if there(t - 2):
                    s = t - 2
                    at_least(act, yT_ps, i - 1)
                    hold(act, held, rstd2, s + 1)
                    nc.scalar.activation(yhat[:, u:u + 1], xres[:, bass.ds(s, 1), :], ACT.Identity,
                                         bias=nm2[:], scale=rs2[:]).then_inc(yhat_in, 1)
                if u == 0 and there(i - 1, IT):
                    state_high(i - 1)
                if u == 0 and there(k, IT) and not slot_is(i, IT):
                    at_least(act, state_in, IB + k)
                    gate(k, 0)
                if u == 1 and slot_is(i, IT):
                    last_high(1)
                if there(t - 1):
                    s, v = t - 1, 1 - u
                    at_least(act, attn_ps, s - 1)
                    at_least(act, ctxT_ps, s + 1)
                    nc.scalar.activation(ctxnT[:, v].rearrange("p k n -> p (k n)"), o_ps[:, 0:KD * P],
                                         ACT.Copy).then_inc(ctxT_in, 1)
                if u == 1 and there(k, IT):
                    gate(k, 2)
                if u == 0 and slot_is(i, IT):
                    at_least(act, state_in, IB + k)
                    gate(k, 0)
                if u == 0 and there(i + 1, IT):
                    at_least(act, score_ps, 2 * i + 2)
                    at_least(act, q_ps, i + 2)
                    for m in range(KD):
                        qa = nc.scalar.activation(qT[:, m].rearrange("p u n -> p (u n)"),
                                                  c_ps[:, m * 2 * P:(m + 1) * 2 * P], ACT.Identity,
                                                  bias=col[:, 0, m:m + 1])
                    qa.then_inc(q_in, 1)
                if u == 1 and slot_is(i, IT):
                    gate(k, 3)
                if u == 0 and slot_is(i, 0):
                    act.wait_ge(ffn_come, 16)
                    for n in range(8):
                        nc.scalar.activation(wfh[:, n], wf[:, n], ACT.Copy).then_inc(wfh_in, 1)
                if u == 1 and slot_is(i, IT - 1):
                    last_high(0)
                if u == 0 and slot_is(i, IT):
                    tanhs(0)

            def last_high(j):
                act.wait_ge(state_in, IT + j + 1)
                if j == 1:
                    act.wait_ge(u_ps, 1)
                elif j == 2:
                    act.wait_ge(gate_ps, 4 * (IT - 2) + 3)
                elif j == 3:
                    act.wait_ge(last_parts, 1)
                nc.scalar.activation(state_h[:, PART[j]], state[:, :, j * 2 * P:(j + 1) * 2 * P], ACT.Copy
                                     ).then_inc(last_h_in, 1)

            pipeline(act, slot, FIRST, LAST, BEGIN, END)

            act.wait_ge(gate_ps, 4 * (IT - 1))
            act.wait_ge(yT_ps, IT)
            nc.scalar.activation(yTh[:].rearrange("p k u n -> p (k u n)"), pt_ps[0][:], ACT.Copy
                                 ).then_inc(yT_in, 1)
            last_high(2)
            tanhs(1)
            act.wait_ge(state_in, IB + IT - 1)
            gate(IT - 1, 0)
            gate(IT - 1, 1)
            gate(IT - 1, 2)
            last_high(3)
            gate(IT - 1, 3)
            for j in range(2, IB):
                tanhs(j)

        @block.tensor
        def _(pe):
            mm = nc.tensor.matmul
            pe.wait_ge(ctx_come, 32)
            for m in range(KD):
                for k in range(KD):
                    last = mm(pt_ps[m][:, 0:B * NK], wkv[:, 0, k, m * P:(m + 1) * P], ctx_in[:, k],
                              start=(k == 0), stop=(k == KD - 1))
                last.then_inc(keys_ps, 1)
            for b in range(B):
                for k in range(KD):
                    last = mm(setup_banks[b // 2][0:NK, b % 2 * D:(b % 2 + 1) * D],
                              ctx_in[:, k, b * NK:(b + 1) * NK], wkv[:, 1, k, :],
                              start=(k == 0), stop=(k == KD - 1))
                if b % 2:
                    last.then_inc(vals_ps, 1)
            pe.wait_ge(keys_sb, KD)
            pe.wait_ge(pool_set, 9)
            pe.wait_ge(row_set, 2)

            def set_up_values():
                pe.wait_ge(dve_set, 7)
                pe.wait_ge(vals_sb, B // 2)
                for c in range(KC):
                    h0, nh = chunk_heads(c)
                    if c >= 3:
                        pe.wait_ge(vrow_sb, c - 2)
                    mm(setup_banks[c % 3][0:rows(c), 0:B * nh * DH], sel[:, c * P:c * P + rows(c)],
                       vals[:, :, h0 * DH:(h0 + nh) * DH], start=True, stop=True).then_inc(vrow_ps, 1)

            def transposes(s, u, groups):
                for g in groups:
                    at_least(pe, probT_in, 3 * s + (g == 2))
                    for c in range(4 * g, min(4 * g + 4, KC)):
                        last = nc.tensor.transpose(pt_ps[(u + g) % 2][0:rows(c), (c % 4) * P:(c % 4 + 1) * P],
                                                   kept[:, 1 - u].rearrange("p h n -> p (h n)")
                                                   [:, c * P:c * P + rows(c)], ident[:])
                    last.then_inc(probT_ps, 1)

            def of_state(k, g, m):
                return [(w[:, 2 * g + 1, kk, m * P:(m + 1) * P],
                         part[:, bass.ds(k % 2, 1), kk].rearrange("p o n -> p (o n)"))
                        for w, part in ((wfh, state_h), (wfh, state_l), (wfl, state_h)) for kk in range(KD)]

            def of_input(g, m, factors):
                return [(w[:, 2 * g, kk, m * P:(m + 1) * P], part[:, kk].rearrange("p u n -> p (u n)"))
                        for w, part in factors for kk in range(KD)]

            with_high, with_low = ((wfh, yTh), (wfl, yTh)), ((wfh, yTl),)

            def gate(k, g, chunks):
                for m in chunks:
                    dst = gate_bank(k, g)[:, m * 2 * P:(m + 1) * 2 * P]
                    products(dst, of_state(k, g, m) + of_input(g, m, with_high), stop=False)
                    if g == 0 and m == 0:
                        at_least(pe, yTl_in, k + 1)
                    done = products(dst, of_input(g, m, with_low), start=False)
                if chunks[-1] == KD - 1:
                    done.then_inc(gate_ps, 1)

            def products(dst, terms, start=True, stop=True, **checks):
                for n, (a, b) in enumerate(terms):
                    last = mm(dst, a, b, start=start and n == 0, stop=stop and n == len(terms) - 1, **checks)
                return last

            def turn_yhat(k):
                at_least(pe, yhat_in, 2 * k + 2)
                for uu in range(2):
                    for m in range(KD):
                        last = nc.tensor.transpose(pt_ps[0][:, m * 2 * P + uu * P:m * 2 * P + (uu + 1) * P],
                                                   yhat[:, uu, m * P:(m + 1) * P], ident[:])
                last.then_inc(yT_ps, 1)

            def out_input():
                for uu in range(2):
                    last = products(c_ps[:, uu * D:(uu + 1) * D],
                                    [(part[:, kk, uu], w[:, 6, kk, :]) for kk in range(KD)
                                     for w, part in ((wfh, yTh), (wfh, yTl), (wfl, yTh))])
                last.then_inc(gate_ps, 1)

            def out_state(j):
                pe.wait_ge(last_l_in, j + 1)
                if j == 0:
                    pe.wait_ge(gate_done, 4 * (IT - 3) + 3)
                elif j == 1:
                    pe.wait_ge(x2_in, T)
                else:
                    pe.wait_ge(gate_done, 4 * (IT - 2) + 3)
                for uu in range(2):
                    last = products(state_bank(j)[:, uu * D:(uu + 1) * D],
                                    [(part[:, PART[j], kk, uu * P:(uu + 1) * P], w[:, 7, kk, :]) for kk in range(KD)
                                     for w, part in ((wfh, state_h), (wfh, state_l), (wfl, state_h))])
                last.then_inc(u_ps, 1)

            def masks(i, v):
                at_least(pe, raw_in, 2 * i + 2 + v)
                for a in range(3):
                    n = min(HB, H - HB * a)
                    mm(s_ps[:, a, 0:n * NK], first_row[:],
                       mbias[:, bass.ds((i + 1) // IB, 1), :].broadcast_to([P, n, NK]), start=True, stop=True)

            def scores(i, v):
                at_least(pe, q_in, i + 2)
                for h0, h1 in ((0, HB), (HB, HC), (HC, 2 * HB), (2 * HB, H)):
                    m = h0 // HC
                    o = h0 % HB if h0 < 2 * HB else 0
                    last = mm(s_ps[:, h0 // HB, o * NK:(o + h1 - h0) * NK], qT[:, m, v],
                              kbd[:, bass.ds((i + 1) // IB, 1), m, h0 - m * HC:h1 - m * HC, :]
                              .rearrange("p b h n -> p (b h n)"), start=False, stop=True,
                              skip_group_check=True)
                last.then_inc(score_ps, 1)

            def slot(i, u):
                t = 2 * i + u
                k = i - 2
                if u == 0 and there(t + 1):
                    scores(i - 1, 1)
                if u == 0 and slot_is(i, IT):
                    out_state(0)
                if there(t + 3):
                    s = t + 3
                    at_least(pe, xhat_in, s + 1)
                    at_least(pe, probT_in, 3 * (t - 1), 3 * T)
                    at_least(pe, yT_in, k + u, IT)
                    at_least(pe, xT_in, s - 1)
                    for m in range(KD):
                        last = nc.tensor.transpose(pt_ps[1 - u][:, m * P:(m + 1) * P],
                                                   xhat[:, 1 - u, m * P:(m + 1) * P], ident[:])
                    last.then_inc(xT_ps, 1)
                if u == 1 and there(t + 1):
                    if slot_is(i, -1):
                        pe.wait_ge(kbd_set, KD)
                        pe.wait_ge(dve_set, 5)
                    if not (isinstance(i, int) and (i + 1) // IB == 0):
                        at_least(pe, kbd_set, KD * B)
                    masks(i, 0)
                    scores(i, 0)
                if u == 1 and slot_is(i, -1):
                    set_up_values()
                if there(t - 1):
                    at_least(pe, mag_in, t)
                    if u == 0:
                        at_least(pe, yT_in, k + 1, IT)
                    transposes(t - 1, u, (0,))
                if there(k, IT):
                    if u == 0:
                        at_least(pe, yT_in, k + 1)
                        at_least(pe, wfl_in, 8)
                        at_least(pe, state_l_in, k + 1)
                        if own_banks(k):
                            pe.wait_ge(raw_in, T)
                        else:
                            at_least(pe, gate_done, 4 * k - 1)
                        gate(k, 0, (0,))
                    else:
                        if not own_banks(k):
                            at_least(pe, gate_done, 4 * k + 1)
                        gate(k, 1, (0, 1))
                if there(t - 1):
                    at_least(pe, xT_in, t + 4, T)
                    transposes(t - 1, u, (1, 2))
                if there(t - 1):
                    s, v = t - 1, 1 - u
                    b = i // IB if u == 1 else (i - 1) // IB
                    at_least(pe, ctxn_in, s)
                    if u == 1:
                        at_least(pe, q_in, i + 2, IT)
                    else:
                        at_least(pe, gate_done, 4 * k)
                    for c in range(KC):
                        h0, nh = chunk_heads(c)
                        if c % 4 == 0:
                            at_least(pe, probT_in, 3 * s + c // 4 + 1)
                        last = mm(c_ps[:, h0 * (DH + 1):(h0 + nh) * (DH + 1)], probT[0:rows(c), v, c],
                                  vbd[0:rows(c), bass.ds(b, 1), c, 0:nh * (DH + 1)]
                                  .rearrange("p b n -> p (b n)"),
                                  start=(c == 0), stop=(c == KC - 1), skip_group_check=True)
                    last.then_inc(ctx_ps, 1)
                if there(k, IT):
                    if u == 0:
                        gate(k, 0, (1,))
                    else:
                        if not own_banks(k):
                            at_least(pe, gate_done, 4 * k + 2)
                        gate(k, 2, (0, 1))
                if there(t - 1):
                    s, v = t - 1, 1 - u
                    at_least(pe, x2_in, s)
                    at_least(pe, ctxn_in, s + 1)
                    for m in range(KD):
                        last = nc.tensor.transpose(o_ps[:, m * P:(m + 1) * P], ctxn[:, v, m * P:(m + 1) * P],
                                                   ident[:])
                    last.then_inc(ctxT_ps, 1)
                if u == 0 and there(i + 1, IT):
                    at_least(pe, xT_in, 2 * i + 4)
                    at_least(pe, ctxn_in, t, T)
                    at_least(pe, gate_done, 4 * k)
                    if slot_is(i, -1):
                        pe.wait_ge(wqo_come, 16)
                    if slot_is(i, 0):
                        pe.wait_ge(vrow_sb, KC)
                    for m in range(KD):
                        for kk in range(KD):
                            last = mm(c_ps[:, m * 2 * P:(m + 1) * 2 * P], wa[:, 0, kk, m * P:(m + 1) * P],
                                      xT[:, kk].rearrange("p u n -> p (u n)"), start=(kk == 0),
                                      stop=(kk == KD - 1))
                    last.then_inc(q_ps, 1)
                if u == 1 and there(t + 2):
                    masks(i, 1)
                if u == 1 and there(k + 1, IT) and not slot_is(i, IT):
                    at_least(pe, probT_in, 3 * t, 3 * T)
                    at_least(pe, xT_in, t + 4, T)
                    turn_yhat(k + 1)
                if there(t - 1):
                    s, v = t - 1, 1 - u
                    at_least(pe, ctxT_in, s + 1)
                    for m in range(KD):
                        last = mm(o_ps[:, D:2 * D], ctxnT[:, v, m], wa[:, 1, m, :], start=(m == 0),
                                  stop=(m == KD - 1))
                    last.then_inc(attn_ps, 1)
                if u == 1 and there(k, IT):
                    at_least(pe, ctxn_in, t, T)
                    at_least(pe, q_in, i + 2, IT)
                    out_input()

            pipeline(pe, slot, FIRST, LAST, BEGIN, END)

            last_k = IT - 1
            pe.wait_ge(probT_in, 3 * T)
            pe.wait_ge(yT_in, last_k)
            turn_yhat(last_k)
            out_state(1)
            pe.wait_ge(state_l_in, IT)
            pe.wait_ge(u_in, 1)
            for g in range(3):
                for m in range(KD):
                    done = products(gate_bank(last_k, g)[:, m * 2 * P:(m + 1) * 2 * P],
                                    of_state(last_k, g, m), start=(m == 0), stop=False,
                                    skip_group_check=True)
            done.then_inc(last_parts, 1)
            pe.wait_ge(yT_in, IT)
            for g in range(3):
                for m in range(KD):
                    products(gate_bank(last_k, g)[:, m * 2 * P:(m + 1) * 2 * P],
                             of_input(g, m, with_high), start=False, stop=False, skip_group_check=True)
                pe.wait_ge(yTl_in, IT)
                for m in range(KD):
                    done = products(gate_bank(last_k, g)[:, m * 2 * P:(m + 1) * 2 * P],
                                    of_input(g, m, with_low), start=False, skip_group_check=True)
                done.then_inc(gate_ps, 1)
            out_state(2)
            pe.wait_ge(gate_done, 4 * last_k)
            out_input()
            out_state(3)


def kernel(**inputs):
    import numpy as _np
    import concourse.bacc as _bacc
    from concourse import mybir as _mybir
    from concourse.bass_utils import run_bass_kernel_spmd as _run

    def get(name):
        return _np.asarray(inputs[name])

    def tr(name):
        return get(name).T

    cols = ["L0_xattn_wq_b", "L0_xattn_wk_b", "L0_ffn_bf", "L0_ffn_bi", "L0_ffn_bc", "L0_ffn_bo", "L0_ffn_in_c"]
    arrays = {
        "x": get("x"),
        "ctxT": get("ctx_1024")[:, ::-1].transpose(2, 0, 1).reshape(256, 4 * 77),
        "mask": _np.broadcast_to(get("mask_BxS2_bf1").view(_np.uint8)[:, ::-1].reshape(1, -1), (128, 4 * 77)),
        "w_attn": _np.stack([tr(f"L0_xattn_w{n}_w") for n in "kvqo"]),
        "w_ffn": _np.stack([tr(f"L0_ffn_{m}{n}") for n in "fico" for m in "wu"]),
        "cols": _np.stack([get(n) for n in cols]).reshape(7, 2, 128).transpose(2, 0, 1).reshape(128, 14),
        "brows": _np.broadcast_to(_np.stack([get("L0_xattn_wv_b"), get("L0_xattn_wo_b"), get("L0_ffn_bo")]), (128, 3, 256)),
        "gates": _np.broadcast_to(_np.concatenate([get("g_xattn"), get("g_ffn")]), (128, 2)),
    }
    arrays = {f"{n}_dram": _np.ascontiguousarray(a) for n, a in arrays.items()}
    nc = _bacc.Bacc("TRN2", target_bir_lowering=False, num_devices=1)
    args = [nc.dram_tensor(n, a.shape, _mybir.dt.from_np(a.dtype), kind="ExternalInput").ap()
            for n, a in arrays.items()]
    out = nc.dram_tensor("out_dram", (4, 1024, 256), _mybir.dt.float32, kind="ExternalOutput").ap()
    build(nc, *args, out)
    r = _run(nc, [arrays], core_ids=[0])
    return r.results[0]["out_dram"]
```
